# Optimizing a Trainium2 kernel written in Bass

```python
import numpy as np
import jax
import jax.numpy as jnp

def _softmax(x, axis=-1):
    return jax.nn.softmax(x, axis=axis)

def _gelu(x):
    return jax.nn.gelu(x, approximate=True)

def _silu(x):
    return jax.nn.silu(x)

def _sigmoid(x):
    return jax.nn.sigmoid(x)

def _layernorm(x, axis=-1, eps=1e-05):
    m = jnp.mean(x, axis=axis, keepdims=True)
    v = jnp.var(x, axis=axis, keepdims=True)
    return (x - m) / jnp.sqrt(v + eps)

def _scatter_add(tgt, idx, src, axis=0):
    return tgt.at[idx].add(src)

def _segment_sum(src, seg, n):
    return jax.ops.segment_sum(src, seg, n)
kernel_name = 'mk_cond_resid_d2_seqx_r4_38e995'

def setup_inputs(seed: int=0):
    np.random.seed(seed)
    _w = jnp.asarray

    def _rec_inputs():
        import jax
        import jax.numpy as jnp
        _rk = jax.random.key(seed)
        x = 7.22e-05 + 1 * jax.random.normal(jax.random.fold_in(_rk, 1), (16, 256, 512), jnp.float32)
        _lenS = 256 - jax.random.randint(jax.random.fold_in(_rk, 7), (16,), 0, max(1, 256 // 4) + 1, jnp.int32)
        _lenS2 = 256 - jax.random.randint(jax.random.fold_in(_rk, 8), (16,), 0, max(1, 256 // 4) + 1, jnp.int32)
        cond_2048 = jax.random.bernoulli(jax.random.fold_in(_rk, 11), 0.5063, (16, 512)).astype(jnp.float32)
        return (x, cond_2048)
    x, cond_2048 = _rec_inputs()

    def _L0_cond_setup():
        import jax, jax.numpy as jnp
        import numpy as np
        NH = 8
        NEG = -1e+30
        key = jax.random.key(seed)
        k1, k2, k3, k4 = jax.random.split(key, 4)
        B, D, T = (4, 256, 512)
        x = jax.random.normal(k1, (B, D, T), dtype=jnp.float32)
        mask = jax.random.randint(k2, (B, T), 0, 2).astype(jnp.float32)
        lim = float(np.sqrt(6.0 / (D + D)))
        Wq = jax.random.uniform(k3, (D, D), dtype=jnp.float32, minval=-lim, maxval=lim)
        Wo = jax.random.uniform(k4, (D, D), dtype=jnp.float32, minval=-lim, maxval=lim)
        return {'x': x, 'mask': mask, 'Wq': Wq, 'Wo': Wo}
    _L0_cond_all = _L0_cond_setup()
    _L0_cond_in = {k: v for k, v in _L0_cond_all.items() if k in ('Wq', 'Wo')}
    del _L0_cond_all

    def _L1_cond_setup():
        import jax, jax.numpy as jnp
        import numpy as np
        HEADS = 16
        EPS = 1e-06

        def _rms_norm(x, g):
            xf = x.astype(jnp.float32)
            y = xf * jax.lax.rsqrt(jnp.mean(xf * xf, axis=-1, keepdims=True) + EPS)
            return y.astype(x.dtype) * g
        key = jax.random.key(seed)
        ks = jax.random.split(key, 6)
        b, n, dim, emb_dim = (4, 512, 512, 512)
        d_head = dim // HEADS
        return {'x': jax.random.normal(ks[0], (b, n, dim), jnp.float32), 'emb': jax.random.normal(ks[1], (b, 1, emb_dim), jnp.float32), 'W_emb': jax.random.normal(ks[2], (emb_dim, 2 * dim), jnp.float32) * emb_dim ** (-0.5), 'b_emb': jnp.zeros((2 * dim,), jnp.float32), 'g_norm': jnp.ones((dim,), jnp.float32), 'W_qkv': jax.random.normal(ks[3], (dim, 3 * dim), jnp.float32) * dim ** (-0.5), 'g_q': jnp.ones((d_head,), jnp.float32), 'g_k': jnp.ones((d_head,), jnp.float32), 'W_out': jax.random.normal(ks[4], (dim, dim), jnp.float32) * dim ** (-0.5)}
    _L1_cond_all = _L1_cond_setup()
    _L1_cond_in = {k: v for k, v in _L1_cond_all.items() if k in ('W_emb', 'b_emb', 'g_norm', 'W_qkv', 'g_q', 'g_k', 'W_out')}
    del _L1_cond_all
    return {'x': x, 'cond_2048': cond_2048, 'L0_cond_Wq': _L0_cond_in['Wq'], 'L0_cond_Wo': _L0_cond_in['Wo'], 'L1_cond_W_emb': _L1_cond_in['W_emb'], 'L1_cond_b_emb': _L1_cond_in['b_emb'], 'L1_cond_g_norm': _L1_cond_in['g_norm'], 'L1_cond_W_qkv': _L1_cond_in['W_qkv'], 'L1_cond_g_q': _L1_cond_in['g_q'], 'L1_cond_g_k': _L1_cond_in['g_k'], 'L1_cond_W_out': _L1_cond_in['W_out']}

def reference(x, cond_2048, L0_cond_Wq, L0_cond_Wo, L1_cond_W_emb, L1_cond_b_emb, L1_cond_g_norm, L1_cond_W_qkv, L1_cond_g_q, L1_cond_g_k, L1_cond_W_out):
    import jax
    import jax.numpy as jnp

    def _L0_cond_ref(x, mask, Wq, Wo):
        import jax, jax.numpy as jnp
        import numpy as np
        NH = 8
        NEG = -1e+30
        B, D, T = x.shape
        dk = D // NH
        scale = 1.0 / jnp.sqrt(jnp.asarray(dk, x.dtype))
        xt = jnp.transpose(x, (0, 2, 1))
        q = xt @ Wq.T
        qh = q.reshape(B, T, NH, dk).transpose(0, 2, 1, 3)
        scores = scale * jnp.einsum('bhqd,bhkd->bhqk', qh, qh)
        cmask = mask[:, None, None, :]
        rmask = mask[:, None, :, None]
        logits = (scores * cmask + (1.0 - cmask) * NEG) * rmask
        attn = jax.nn.softmax(logits, axis=-1)
        ctx = jnp.einsum('bhqk,bhkd->bhqd', attn, qh)
        ctx = ctx.transpose(0, 2, 1, 3).reshape(B, T, D)
        out = ctx @ Wo.T
        return jnp.transpose(out, (0, 2, 1))

    def _L1_cond_ref(x, emb, W_emb, b_emb, g_norm, W_qkv, g_q, g_k, W_out):
        import jax, jax.numpy as jnp
        import numpy as np
        HEADS = 16
        EPS = 1e-06

        def _rms_norm(x, g):
            xf = x.astype(jnp.float32)
            y = xf * jax.lax.rsqrt(jnp.mean(xf * xf, axis=-1, keepdims=True) + EPS)
            return y.astype(x.dtype) * g
        b, n, dim = x.shape
        h = HEADS
        d = dim // h
        scale_shift = emb @ W_emb + b_emb
        scale, shift = jnp.split(scale_shift, 2, axis=-1)
        xn = _rms_norm(x, g_norm) * (1.0 + scale) + shift
        qkv = xn @ W_qkv
        qkv = qkv.reshape(b, n, 3, h, d)
        q, k, v = jnp.moveaxis(qkv, 2, 0)
        q = jnp.swapaxes(q, 1, 2)
        k = jnp.swapaxes(k, 1, 2)
        v = jnp.swapaxes(v, 1, 2)
        q = _rms_norm(q, g_q)
        k = _rms_norm(k, g_k)
        logits = jnp.einsum('bhqd,bhkd->bhqk', q, k) * d ** (-0.5)
        attn = jax.nn.softmax(logits, axis=-1)
        o = jnp.einsum('bhqk,bhkd->bhqd', attn, v)
        o = jnp.swapaxes(o, 1, 2).reshape(b, n, dim)
        return o + o @ W_out
    x = x + _L0_cond_ref(x, cond_2048, L0_cond_Wq, L0_cond_Wo)
    x = x + _L1_cond_ref(x, cond_2048[:, None, :], L1_cond_W_emb, L1_cond_b_emb, L1_cond_g_norm, L1_cond_W_qkv, L1_cond_g_q, L1_cond_g_k, L1_cond_W_out)
    return x

_drawn_inputs = setup_inputs


def setup_inputs(seed=0):
    import zlib

    import numpy as np

    out = dict(_drawn_inputs(seed))
    spreads = {'L1_cond_b_emb': (0.0, 0.1),
     'L1_cond_g_norm': (1.0, 0.2),
     'L1_cond_g_q': (1.0, 0.592),
     'L1_cond_g_k': (1.0, 0.6)}
    factors = {}
    for name, (base, spread) in spreads.items():
        noise = np.random.default_rng([zlib.crc32(name.encode()), seed]).standard_normal(out[name].shape)
        drawn = base * np.exp(spread * noise) if base else spread * noise
        out[name] = jnp.asarray(drawn.astype(out[name].dtype))
    for name, factor in factors.items():
        out[name] = (out[name] * factor).astype(out[name].dtype)
    return out
```

```python
from contextlib import ExitStack

import numpy as np

import concourse.bass as bass
from concourse import mybir

F32 = mybir.dt.float32
F32R = mybir.dt.float32r
ALU = mybir.AluOpType
ACT = mybir.ActivationFunctionType
AX = mybir.AxisListType

NB = 16
P = 128
D0, T0 = 256, 512
N1, DM = 256, 512
DH = 32
H0, H1 = D0 // DH, DM // DH
QH = 4
Q0, Q1 = H0 // QH, H1 // QH
KB0, KB1 = T0 // P, N1 // P
SCALE = float(DH) ** -0.5
EPS = 1e-6
NEG = 1e30

MAX_IN = {"A": (6, 5, 5, 0), "B": (0, 5, 5, 6), "C": (6, 5, 5, 0)}


LOOP = (3, NB - 1)


def units(seg, g):
    first = sum(MAX_IN[seg][:g])
    return range(first, first + MAX_IN[seg][g])


class Event:

    def __init__(self, sem, per):
        self.sem, self.per = sem, per

    def at(self, b, n=None):
        n = self.per if n is None else n
        if not isinstance(b, int):
            return b * self.per + n
        return max(0, min(b * self.per + n, NB * self.per))


class Turns:

    def __init__(self, n, uses):
        self.n, self.uses = n, uses
        self.place = {key: k for k, (key, _) in enumerate(uses)}

    def slot(self, key):
        return self.place[key] % self.n

    def _count(self, key, i, mine):
        def upto(i):
            n = 0
            for j in range(-1, i + 1):
                for k, (_, off) in enumerate(self.uses):
                    if (j < i or k <= self.place[key]) and 0 <= j + off < NB and mine(k):
                        n += 1
            return n
        if isinstance(i, int):
            return upto(i)
        per = upto(LOOP[0] + 1) - upto(LOOP[0])
        return i * per + (upto(LOOP[0]) - LOOP[0] * per)

    def nth(self, key, i):
        return self._count(key, i, lambda k: True)

    def nth_of_slot(self, key, i):
        return self._count(key, i, lambda k: k % self.n == self.slot(key))


def before(count, n):
    return max(0, count - n) if isinstance(count, int) else count - n


def cond_resid(nc, x, cond, cond_t, wq_t, wo_t, w_emb, b_emb_t, g_norm_t, w_qkv, g_q_t, g_k_t, w_out, out):
    x_v = x.rearrange("b (c p) t -> b p c t", p=P)
    out_v = out.rearrange("b (c p) t -> b p c t", p=P)
    ctx = ExitStack()
    with ctx:
        def sb(name, shape, dt=F32):
            return ctx.enter_context(nc.sbuf_tensor(name, shape, dt))

        def pb(name, shape):
            return ctx.enter_context(nc.psum_tensor(name, shape, F32))

        def ev(name, per):
            return Event(ctx.enter_context(nc.semaphore(name)), per)

        WQ = sb("WQ", [P, 2, D0])
        WO = sb("WO", [P, 2, D0])
        WQKV = sb("WQKV", [P, 4, 3 * DM])
        WOUT = sb("WOUT", [P, 4, DM])
        CT = sb("CT", [P, 4, NB])
        KBIAS = sb("KBIAS", [P, 4, NB])
        KCOL = sb("KCOL", [P, 4])
        BEMB = sb("BEMB", [P, 8])
        GN = sb("GN", [P, 4])
        GQK = sb("GQK", [P, 2])
        AMOD = sb("AMOD", [P, 4, NB])
        SMOD = sb("SMOD", [P, 4, NB])
        IDENT = sb("IDENT", [P, P])
        ONES = sb("ONES", [P, DH])
        A0 = sb("A0", [P, H0, T0], F32R)
        B0 = sb("B0", [P, H0, T0], F32R)
        XIN = sb("XIN", [P, 2, T0])
        CBM = sb("CBM", [P, T0])
        CBR = sb("CBR", [P, T0])
        XMC = sb("XMC", [P, 2, T0])
        XS = sb("XS", [P, 2])
        MEAN = sb("MEAN", [P, 2, NB])
        QHI = sb("QHI", [P, 2, T0], F32R)
        QLO = sb("QLO", [P, 2, T0], F32R)
        QF = sb("QF", [P, 2, T0])
        OUTT = QF
        V0 = sb("V0", [P, 2, KB0, P])
        NM0 = sb("NM0", [P, 2, 16])
        NMT0 = sb("NMT0", [16, 2, P], F32R)
        A1 = sb("A1", [P, QH, Q1, N1], F32R)
        B1 = sb("B1", [P, QH, Q1, N1], F32R)
        X1 = sb("X1", [P, 2, DM])
        X1R = sb("X1R", [P, 2, DM])
        SS = sb("SS", [P, 2])
        RSTD = sb("RSTD", [P, 2])
        YSQ = sb("YSQ", [P, 2, DM])
        XNT = sb("XNT", [P, 4, N1])
        QK = sb("QK", [P, 2, 2 * DM])
        SSQ = sb("SSQ", [P, 2, 2 * H1])
        RQK = sb("RQK", [P, 2, 2 * H1])
        HALF = sb("HALF", [P, 2 * H1])
        KQHI = sb("KQHI", [P, 2, Q1, N1], F32R)
        KQLO = sb("KQLO", [P, 2, Q1, N1], F32R)
        V1 = sb("V1", [P, 2, DM])
        NM1 = sb("NM1", [P, 2 * H1])
        NMT1 = sb("NMT1", [2 * H1, P], F32R)
        R1 = sb("R1", [P, N1])
        OT = sb("OT", [P, Q1, N1])
        E = sb("E", [P, 2, QH, T0])
        WEMB = E[:, :, :, :].rearrange("p a h t -> p (a h t)").rearrange("p (c n) -> p c n", c=4)
        R0 = QK[:, 0, 0:T0]
        TT = QK[:, 0, T0:2 * T0]
        CINV = QK[:, 1, 0:T0]

        PM = [pb(f"PM{k}", [P, 512]) for k in range(2)]
        PS = [pb(f"PS{k}", [P, 512]) for k in range(2)]
        PO = pb("PO", [P, 512])
        PD = pb("PD", [P, 512])
        PX = [pb(f"PX{k}", [P, 512]) for k in range(2)]

        weights_in = ev("weights_in", 0)
        consts_set = ev("consts_set", 0)
        ident_set = ev("ident_set", 0)
        mod_full = ev("mod_full", 0)
        mod_done = ev("mod_done", 0)
        xin_in = ev("xin_in", 16)
        cbm_in = ev("cbm_in", 16)
        cbr_in = ev("cbr_in", 16)
        xres_in = ev("xres_in", 16)
        xm_done = ev("xm_done", 2)
        xs_done = ev("xs_done", 1)
        p0_full = ev("p0_full", 3)
        qhi_done = ev("qhi_done", 2)
        qf_done = ev("qf_done", 2)
        stack0_in = [ev(f"stack0_in{q}", 24 * 16) for q in range(Q0)]
        t0_full = ev("t0_full", 2)
        m0_full = ev("m0_full", 32)
        n0_full = ev("n0_full", 2)
        row0_in = [ev(f"row0_in{q}", 16) for q in range(Q0)]
        s0_full = ev("s0_full", 32)
        kcol_done = ev("kcol_done", 1)
        cinv_done = ev("cinv_done", 1)
        dd_done = ev("dd_done", 2)
        recip0_done = ev("recip0_done", 2)
        rc_done = ev("rc_done", 2)
        m_done = ev("m_done", 2)
        ctx_done = ev("ctx_done", 2)
        w0_full = ev("w0_full", 2)
        ss_done = ev("ss_done", 2)
        ms_done = ev("ms_done", 1)
        rstd_done = ev("rstd_done", 1)
        y_done = ev("y_done", 2)
        x1r_done = ev("x1r_done", 1)
        t1_full = ev("t1_full", 2)
        p1_full = ev("p1_full", 4)
        v1_full = ev("v1_full", 2)
        sq_done = ev("sq_done", 2)
        ssq_done = ev("ssq_done", 2)
        msq_done = ev("msq_done", 2)
        rqk_done = ev("rqk_done", 2)
        qn_done = ev("qn_done", 2)
        tq_full = ev("tq_full", 4)
        kqhi_done = ev("kqhi_done", 4)
        stack1_in = ev("stack1_in", 24 * 16)
        m1_full = ev("m1_full", 16)
        n1_full = ev("n1_full", 1)
        row1_in = ev("row1_in", 16)
        s1_full = ev("s1_full", 16)
        recip1_done = ev("recip1_done", 4)
        w1_full = ev("w1_full", 2)
        stored = ev("stored", 16)
        max_done = ctx.enter_context(nc.semaphore("max_done"))
        exp_done = ctx.enter_context(nc.semaphore("exp_done"))
        pv_done = ctx.enter_context(nc.semaphore("pv_done"))
        context_taken = ctx.enter_context(nc.semaphore("context_taken"))
        other_taken = [ctx.enter_context(nc.semaphore(f"other_taken{k}")) for k in range(2)]

        maxima = Turns(2, [(("A", u), 0) for u in range(16)] + [(("B", u), -1) for u in range(16)]
                       + [(("C", u), 1) for u in range(16)])
        scores = Turns(2, [(("A", u), 0) for u in range(16)] + [(("B", u), 0) for u in range(16)]
                       + [(("C", u), -1) for u in range(16)])
        probs = Turns(2, [(("A", g), 0) for g in range(4)] + [(("B", g), 0) for g in range(4)]
                      + [(("C", g), -1) for g in range(4)])
        context = Turns(1, [("A", 0), ("B", 0)] + [(("C", c), -1) for c in range(4)])
        other = Turns(2, [*[(("p1", k), -1) for k in range(4)], (("w1", 0), -2), (("w1", 1), -2), (("n0", 1), 0),
                          *[(("tq", k), -1) for k in range(4)], (("p0", 0), 1), (("p0", 1), 1), (("mean", 0), 1),
                          (("t0", 0), 1), (("v1", 0), -1), (("n1", 0), -1), (("v1", 1), -1),
                          (("w0", 0), 0), (("w0", 1), 0), (("n0", 0), 1), (("t0", 1), 1),
                          (("t1", 0), 0), (("t1", 1), 0)])

        def has(i, off):
            return not isinstance(i, int) or 0 <= i + off < NB

        def held(eng, count):
            return count if isinstance(count, int) else eng.to_reg(count)

        def taken(key):
            return other_taken[other.slot(key)]

        def pipeline(eng, iteration):
            for i in range(-1, LOOP[0]):
                iteration(i)
            with eng.Fori(*LOOP) as i:
                iteration(i)
            for i in range(LOOP[1], NB + 2):
                iteration(i)

        block = ctx.enter_context(nc.Block())

        @block.tensor
        def _(pe):
            mm, tp = nc.tensor.matmul, nc.tensor.transpose

            def modulation():
                for n in range(8):
                    for c in range(4):
                        last = mm(PX[0][:, n * NB:(n + 1) * NB], WEMB[:, c, n * P:(n + 1) * P], CT[:, c, :],
                                  start=(c == 0), stop=(c == 3))
                last.then_inc(mod_full.sem, 1)

            def project0(i, b):
                pe.wait_ge(xm_done.sem, xm_done.at(b))
                for mt in range(2):
                    pe.wait_ge(taken(("p0", mt)), before(other.nth_of_slot(("p0", mt), i), 1))
                    bank = PX[other.slot(("p0", mt))]
                    for c in range(2):
                        last = mm(bank[:, :], WQ[:, c, mt * P:(mt + 1) * P], XMC[:, c, :], start=(c == 0), stop=(c == 1))
                    last.then_inc(p0_full.sem, 1)
                pe.wait_ge(taken(("mean", 0)), before(other.nth_of_slot(("mean", 0), i), 1))
                pe.wait_ge(xs_done.sem, xs_done.at(b))
                bank = PX[other.slot(("mean", 0))]
                for mt in range(2):
                    for c in range(2):
                        last = mm(bank[:, mt:mt + 1], WQ[:, c, mt * P:(mt + 1) * P], XS[:, c:c + 1],
                                  start=(c == 0), stop=(c == 1))
                last.then_inc(p0_full.sem, 1)

            def values0(i, b, mt):
                pe.wait_ge(taken(("t0", mt)), before(other.nth_of_slot(("t0", mt), i), 1))
                pe.wait_ge(qf_done.sem, qf_done.at(b, mt + 1))
                bank = PX[other.slot(("t0", mt))]
                for kb in range(KB0):
                    last = tp(bank[:, kb * P:(kb + 1) * P], QF[:, mt, kb * P:(kb + 1) * P], IDENT[:, :])
                last.then_inc(t0_full.sem, 1)

            def max0(seg, i, b, q, u):
                h, kb = q * QH + u // KB0, u % KB0
                if u == 0:
                    pe.wait_ge(stack0_in[q].sem, stack0_in[q].at(b))
                pe.wait_ge(max_done, before(maxima.nth((seg, u), i), 2))
                mm(PM[maxima.slot((seg, u))][:, :], A0[0:96, h, kb * P:(kb + 1) * P], B0[0:96, h, :],
                   start=True, stop=True).then_inc(m0_full.sem, 1)

            def max1(i, b, u):
                hq, c = u // Q1, u % Q1
                if u == 0:
                    pe.wait_ge(stack1_in.sem, stack1_in.at(b))
                pe.wait_ge(max_done, before(maxima.nth(("B", u), i), 2))
                bank = PM[maxima.slot(("B", u))]
                for qb in range(2):
                    last = mm(bank[:, qb * N1:(qb + 1) * N1], B1[0:96, hq, c, qb * P:(qb + 1) * P], A1[0:96, hq, c, :],
                              start=True, stop=True)
                last.then_inc(m1_full.sem, 1)

            def rows0(i, b, q):
                pe.wait_ge(taken(("n0", q)), before(other.nth_of_slot(("n0", q), i), 1))
                pe.wait_ge(max_done, maxima.nth(("AC"[q == 0], 15), i))
                tp(PX[other.slot(("n0", q))][0:16, 0:P], NM0[:, q, :], IDENT[:, :]).then_inc(n0_full.sem, 1)

            def rows1(i, b):
                pe.wait_ge(taken(("n1", 0)), before(other.nth_of_slot(("n1", 0), i), 1))
                pe.wait_ge(max_done, maxima.nth(("B", 15), i))
                tp(PX[other.slot(("n1", 0))][0:2 * H1, 0:P], NM1[:, :], IDENT[:, :]).then_inc(n1_full.sem, 1)

            def score0(seg, i, b, q, g, hq):
                u, h = g * QH + hq, q * QH + hq
                if u == 0:
                    pe.wait_ge(row0_in[q].sem, row0_in[q].at(b))
                pe.wait_ge(exp_done, before(scores.nth((seg, u), i), 2))
                mm(PS[scores.slot((seg, u))][:, :], A0[0:97, h, g * P:(g + 1) * P], B0[0:97, h, :],
                   start=True, stop=True).then_inc(s0_full.sem, 1)

            def score1(i, b, c, hq):
                u = c * QH + hq
                if u == 0:
                    pe.wait_ge(row1_in.sem, row1_in.at(b))
                pe.wait_ge(exp_done, before(scores.nth(("C", u), i), 2))
                bank = PS[scores.slot(("C", u))]
                for kb in range(KB1):
                    last = mm(bank[:, kb * N1:(kb + 1) * N1], A1[0:97, hq, c, kb * P:(kb + 1) * P], B1[0:97, hq, c, :],
                              start=True, stop=True)
                last.then_inc(s1_full.sem, 1)

            def context0(seg, i, b, q, g):
                if g == 0:
                    pe.wait_ge(context_taken, before(context.nth(seg, i), 1))
                    pe.wait_ge(taken(("t0", q)), other.nth_of_slot(("t0", q), i - 1))
                pe.wait_ge(exp_done, scores.nth((seg, QH * g + QH - 1), i))
                e = E[:, probs.slot((seg, g)), :, :]
                for bank, ones in ((PO, False), (PD, True)):
                    for h in range(QH):
                        w = ONES[:, :] if ones else V0[:, q, g, h * DH:(h + 1) * DH]
                        last = mm(bank[h * DH:(h + 1) * DH, :], w, e[:, h, :], start=(g == 0), stop=(g == KB0 - 1))
                last.then_inc(pv_done, 1)

            def context1(i, b, c):
                pe.wait_ge(context_taken, before(context.nth(("C", c), i), 1))
                if c == 0:
                    pe.wait_ge(taken(("v1", 1)), other.nth_of_slot(("v1", 1), i))
                pe.wait_ge(exp_done, scores.nth(("C", QH * c + QH - 1), i))
                e = E[:, probs.slot(("C", c)), :, :]
                for bank, ones in ((PO, False), (PD, True)):
                    for kb in range(KB1):
                        for h in range(QH):
                            w = ONES[:, :] if ones else V1[:, kb, c * P + h * DH:c * P + (h + 1) * DH]
                            last = mm(bank[h * DH:(h + 1) * DH, 0:N1], w, e[:, h, kb * N1:(kb + 1) * N1],
                                      start=(kb == 0), stop=(kb == KB1 - 1))
                last.then_inc(pv_done, 1)

            def out0(i, b):
                pe.wait_ge(ctx_done.sem, ctx_done.at(b))
                for mt in range(2):
                    pe.wait_ge(taken(("w0", mt)), before(other.nth_of_slot(("w0", mt), i), 1))
                    bank = PX[other.slot(("w0", mt))]
                    for c in range(2):
                        last = mm(bank[:, :], WO[:, c, mt * P:(mt + 1) * P], XMC[:, c, :], start=(c == 0), stop=(c == 1))
                    last.then_inc(w0_full.sem, 1)

            def norm_rows(i, b):
                pe.wait_ge(y_done.sem, y_done.at(b))
                for k in range(2):
                    pe.wait_ge(taken(("t1", k)), before(other.nth_of_slot(("t1", k), i), 1))
                    bank = PX[other.slot(("t1", k))]
                    for cc in range(2):
                        for t in range(2):
                            c = 2 * k + cc
                            last = tp(bank[:, (2 * cc + t) * P:(2 * cc + t + 1) * P], YSQ[:, t, c * P:(c + 1) * P],
                                      IDENT[:, :])
                    last.then_inc(t1_full.sem, 1)

            def project1(i, b, key, t, part, event):
                pe.wait_ge(taken(key), before(other.nth_of_slot(key, i), 1))
                if key == ("p1", 0):
                    pe.wait_ge(taken(("t1", 1)), other.nth_of_slot(("t1", 1), i - 1))
                bank = PX[other.slot(key)]
                for c in range(4):
                    last = mm(bank[:, :], XNT[:, c, t * P:(t + 1) * P], WQKV[:, c, part * DM:(part + 1) * DM],
                              start=(c == 0), stop=(c == 3))
                last.then_inc(event.sem, 1)

            def heads_rows(i, b):
                pe.wait_ge(qn_done.sem, qn_done.at(b))
                for part in range(2):
                    for k in range(2):
                        key = ("tq", 2 * part + k)
                        pe.wait_ge(taken(key), before(other.nth_of_slot(key, i), 1))
                        bank = PX[other.slot(key)]
                        for cc in range(2):
                            for t in range(2):
                                c = 2 * k + cc
                                last = tp(bank[:, (2 * cc + t) * P:(2 * cc + t + 1) * P],
                                          QK[:, t, part * DM + c * P:part * DM + (c + 1) * P], IDENT[:, :])
                        last.then_inc(tq_full.sem, 1)

            def out1(i, b):
                pe.wait_ge(context_taken, context.nth(("C", 3), b + 1))
                for t in range(2):
                    pe.wait_ge(taken(("w1", t)), before(other.nth_of_slot(("w1", t), i), 1))
                    bank = PX[other.slot(("w1", t))]
                    for c in range(4):
                        last = mm(bank[:, :], OT[:, c, t * P:(t + 1) * P], WOUT[:, c, :], start=(c == 0), stop=(c == 3))
                    last.then_inc(w1_full.sem, 1)

            def group(seg, i, g, s_off, score, m_off, maximum):
                us = list(units(seg, g))
                for k in range(max(QH, len(us))):
                    if k < QH and has(i, s_off):
                        score(g, k)
                    if k < len(us) and has(i, m_off):
                        maximum(us[k])

            def iteration(i):
                def a_group(g):
                    group("A", i, g, 0, lambda g, h: score0("A", i, i, 0, g, h), 0, lambda u: max0("A", i, i, 1, u))
                a_group(0)
                if has(i, -1):
                    for k in range(4):
                        project1(i, i - 1, ("p1", k), k // 2, k % 2, p1_full)
                a_group(1)
                if has(i, 0):
                    context0("A", i, i, 0, 0)
                if has(i, -2):
                    out1(i, i - 2)
                a_group(2)
                if has(i, 0):
                    context0("A", i, i, 0, 1)
                    rows0(i, i, 1)
                if has(i, -1):
                    heads_rows(i, i - 1)
                a_group(3)
                if has(i, 0):
                    context0("A", i, i, 0, 2)
                if has(i, 1):
                    project0(i, i + 1)
                if has(i, 0):
                    context0("A", i, i, 0, 3)

                def b_group(g):
                    group("B", i, g, 0, lambda g, h: score0("B", i, i, 1, g, h), -1, lambda u: max1(i, i - 1, u))
                b_group(0)
                for g in (1, 2, 3):
                    b_group(g)
                    if has(i, 0):
                        context0("B", i, i, 1, g - 1)
                if has(i, 1):
                    values0(i, i + 1, 0)
                if has(i, -1):
                    project1(i, i - 1, ("v1", 0), 0, 2, v1_full)
                if has(i, 0):
                    context0("B", i, i, 1, 3)
                if has(i, -1):
                    rows1(i, i - 1)
                    project1(i, i - 1, ("v1", 1), 1, 2, v1_full)

                def c_group(g):
                    group("C", i, g, -1, lambda g, h: score1(i, i - 1, g, h), 1, lambda u: max0("C", i, i + 1, 0, u))
                c_group(0)
                c_group(1)
                if has(i, -1):
                    context1(i, i - 1, 0)
                if has(i, 0):
                    out0(i, i)
                c_group(2)
                if has(i, -1):
                    context1(i, i - 1, 1)
                if has(i, 1):
                    rows0(i, i + 1, 0)
                    values0(i, i + 1, 1)
                c_group(3)
                if has(i, -1):
                    context1(i, i - 1, 2)
                if has(i, 0):
                    norm_rows(i, i)
                if has(i, -1):
                    context1(i, i - 1, 3)

            pe.wait_ge(weights_in.sem, 16 * 10)
            pe.wait_ge(ident_set.sem, 3)
            pe.wait_ge(consts_set.sem, 4)
            modulation()
            pe.wait_ge(mod_done.sem, 1)
            pipeline(pe, iteration)

        @block.scalar
        def _(act):
            fn = nc.scalar.activation

            def copy(o, i_):
                return fn(o, i_, ACT.Copy)

            def exps0(seg, i, b, q, g):
                if seg == "A" and g == 0:
                    count_0 = held(act, scores.nth(("B", 15), i - 1))
                    act.wait_ge(ident_set.sem, 3)
                    act.wait_ge(exp_done, count_0)
                    copy(KCOL[:, :].unsqueeze(2), KBIAS[:, :, bass.ds(b, 1)]).then_inc(kcol_done.sem, 1)
                    act.wait_ge(kcol_done.sem, kcol_done.at(b))
                act.wait_ge(pv_done, before(probs.nth((seg, g), i), 2))
                for h in range(QH):
                    u = g * QH + h
                    act.wait_ge(s0_full.sem, s0_full.at(b, 16 * q + u + 1))
                    fn(E[:, probs.slot((seg, g)), h, :], PS[scores.slot((seg, u))][:, :], ACT.Exp,
                       bias=KCOL[:, g:g + 1], scale=SCALE).then_inc(exp_done, 1)

            def exps1(i, b, c):
                act.wait_ge(pv_done, before(probs.nth(("C", c), i), 2))
                for h in range(QH):
                    u = c * QH + h
                    act.wait_ge(s1_full.sem, s1_full.at(b, u + 1))
                    fn(E[:, probs.slot(("C", c)), h, :], PS[scores.slot(("C", u))][:, :], ACT.Exp,
                       scale=SCALE).then_inc(exp_done, 1)

            def split0(i, b):
                for mt in range(2):
                    bank = PX[other.slot(("p0", mt))]
                    act.wait_ge(p0_full.sem, p0_full.at(b, mt + 1))
                    act.wait_ge(stack0_in[mt].sem, stack0_in[mt].at(b - 1))
                    copy(QHI[:, mt, :], bank[:, :]).then_inc(qhi_done.sem, 1)
                    act.wait_ge(t0_full.sem, t0_full.at(b - 1, mt + 1))
                    act.wait_ge(stored.sem, stored.at(b - 3))
                    copy(QF[:, mt, :], bank[:, :]).then_inc(qf_done.sem, 1)
                count_0 = held(act, p0_full.at(b, 3))
                act.wait_ge(ident_set.sem, 3)
                act.wait_ge(p0_full.sem, count_0)
                fn(MEAN[:, :, bass.ds(b, 1)], PX[other.slot(("mean", 0))][:, 0:2].rearrange("p (a o) -> p a o", o=1),
                   ACT.Copy, scale=1.0 / T0).then_inc(taken(("mean", 0)), 1)

            def values0(i, b, mt):
                act.wait_ge(t0_full.sem, t0_full.at(b, mt + 1))
                act.wait_ge(pv_done, probs.nth(("AB"[mt], 3), i))
                copy(V0[:, mt, :, :], PX[other.slot(("t0", mt))][:, :].rearrange("p (k d) -> p k d", k=KB0)) \
                    .then_inc(taken(("t0", mt)), 1)

            def rows0(i, b, q):
                act.wait_ge(n0_full.sem, n0_full.at(b, 1 if q == 0 else 2))
                act.wait_ge(row0_in[q].sem, row0_in[q].at(b - 1))
                copy(NMT0[:, q, :], PX[other.slot(("n0", q))][0:16, 0:P]).then_inc(taken(("n0", q)), 1)
                act.wait_ge(taken(("n0", q)), other.nth_of_slot(("n0", q), i))
                act.dma_start(B0[96:97, q * QH:(q + 1) * QH, :].rearrange("p h (k t) -> p (h k) t", t=P).bitcast(F32),
                              NMT0[:, q, :].bitcast(F32)).then_inc(row0_in[q].sem, 16)

            def rows1(i, b):
                act.wait_ge(n1_full.sem, n1_full.at(b))
                act.wait_ge(row1_in.sem, row1_in.at(b - 1))
                copy(NMT1[:, :], PX[other.slot(("n1", 0))][0:2 * H1, 0:P]).then_inc(taken(("n1", 0)), 1)
                act.wait_ge(taken(("n1", 0)), other.nth_of_slot(("n1", 0), i))
                act.dma_start(B1[96:97, :, :, :].rearrange("p h c (k t) -> p (h c k) t", t=P).bitcast(F32),
                              NMT1[:, :].bitcast(F32)).then_inc(row1_in.sem, 16)

            def heads(i, b):
                for k in range(4):
                    act.wait_ge(p1_full.sem, p1_full.at(b, k + 1))
                    if k % 2 == 0:
                        act.wait_ge(ctx_done.sem, ctx_done.at(b))
                        act.wait_ge(qn_done.sem, qn_done.at(b - 1, k // 2 + 1))
                    if k == 0:
                        act.wait_ge(tq_full.sem, tq_full.at(b - 1))
                    copy(QK[:, k // 2, (k % 2) * DM:(k % 2 + 1) * DM], PX[other.slot(("p1", k))][:, :]) \
                        .then_inc(taken(("p1", k)), 1)

            def values1(i, b, t):
                act.wait_ge(v1_full.sem, v1_full.at(b, t + 1))
                act.wait_ge(pv_done, probs.nth(("C", 3), i - 1))
                copy(V1[:, t, :], PX[other.slot(("v1", t))][:, :]).then_inc(taken(("v1", t)), 1)

            def split1(i, b):
                act.wait_ge(stack1_in.sem, stack1_in.at(b - 1))
                for k in range(4):
                    part, half = k // 2, k % 2
                    act.wait_ge(tq_full.sem, tq_full.at(b, k + 1))
                    fn(KQHI[:, part, 2 * half:2 * half + 2, :],
                       PX[other.slot(("tq", k))][:, :].rearrange("p (c t) -> p c t", c=2),
                       ACT.Copy, scale=GQK[:, part:part + 1]).then_inc(kqhi_done.sem, 1)

            def squares(i, b):
                act.wait_ge(ssq_done.sem, ssq_done.at(b - 1))
                act.wait_ge(y_done.sem, y_done.at(b - 1))
                act.wait_ge(t1_full.sem, t1_full.at(b - 1))
                act.wait_ge(ms_done.sem, ms_done.at(b - 1))
                for t in range(2):
                    act.wait_ge(taken(("w0", t)), other.nth_of_slot(("w0", t), i))
                    fn(YSQ[:, t, :], X1[:, t, :], ACT.Square, accum_out=SS[:, t:t + 1]).then_inc(ss_done.sem, 1)

            def iteration(i):
                if has(i, 0):
                    exps0("A", i, i, 0, 0)
                if has(i, -1):
                    heads(i, i - 1)
                if has(i, 0):
                    exps0("A", i, i, 0, 1)
                    exps0("A", i, i, 0, 2)
                    rows0(i, i, 1)
                if has(i, -1):
                    split1(i, i - 1)
                if has(i, 0):
                    exps0("A", i, i, 0, 3)
                if has(i, 1):
                    split0(i, i + 1)
                if has(i, 0):
                    for g in range(4):
                        exps0("B", i, i, 1, g)
                if has(i, 1):
                    values0(i, i + 1, 0)
                if has(i, -1):
                    values1(i, i - 1, 0)
                    rows1(i, i - 1)
                    values1(i, i - 1, 1)
                if has(i, -1):
                    exps1(i, i - 1, 0)
                    exps1(i, i - 1, 1)
                    exps1(i, i - 1, 2)
                if has(i, 0):
                    squares(i, i)
                if has(i, 1):
                    rows0(i, i + 1, 0)
                    values0(i, i + 1, 1)
                if has(i, -1):
                    exps1(i, i - 1, 3)

            act.wait_ge(consts_set.sem, 4)
            act.wait_ge(mod_done.sem, 1)
            pipeline(act, iteration)

        @block.vector
        def _(dve):
            v = nc.vector

            def modulation():
                dve.wait_ge(weights_in.sem, 16 * 10)
                dve.wait_ge(ident_set.sem, 3)
                v.memset(ONES[:, :], 1.0).then_inc(consts_set.sem, 1)
                v.memset(A0[96:97, :, :].bitcast(F32), 1.0).then_inc(consts_set.sem, 1)
                v.memset(A1[96:97, :, :, :].bitcast(F32), 1.0).then_inc(consts_set.sem, 1)
                v.tensor_scalar(KBIAS[:, :, :], CT[:, :, :], 1.0, NEG, ALU.subtract, ALU.mult).then_inc(consts_set.sem, 1)
                for c in range(4):
                    blk = WOUT[:, c, c * P:(c + 1) * P]
                    v.tensor_tensor(blk, blk, IDENT[:, :], ALU.add)
                dve.wait_ge(mod_full.sem, 1)
                for n in range(4):
                    v.tensor_scalar(AMOD[:, n, :], PX[0][:, n * NB:(n + 1) * NB], BEMB[:, n:n + 1], 1.0, ALU.add, ALU.add)
                for n in range(4):
                    last = v.tensor_scalar(SMOD[:, n, :], PX[0][:, (4 + n) * NB:(5 + n) * NB], BEMB[:, 4 + n:5 + n], None,
                                           ALU.add)
                last.then_inc(mod_done.sem, 1)
                dve.wait_ge(mod_done.sem, 1)
                for n in range(4):
                    last = v.tensor_scalar(AMOD[:, n, :], AMOD[:, n, :], GN[:, n:n + 1], None, ALU.mult)
                last.then_inc(mod_done.sem, 1)
                dve.wait_ge(mod_done.sem, 2)

            def sums_x(i, b):
                dve.wait_ge(xin_in.sem, xin_in.at(b))
                dve.wait_ge(p0_full.sem, p0_full.at(b - 1))
                v.reduce_sum(XS[:, :], XIN[:, :, :], AX.X).then_inc(xs_done.sem, 1)

            def max0(seg, i, b, q, us):
                for u in us:
                    if u == 0:
                        dve.wait_ge(n0_full.sem, n0_full.at(b - 1, q + 1))
                    dve.wait_ge(m0_full.sem, m0_full.at(b, 16 * q + u + 1))
                    v.tensor_reduce(NM0[:, q, u:u + 1], PM[maxima.slot((seg, u))][:, :], axis=AX.X, op=ALU.max,
                                    negate=True).then_inc(max_done, 1)

            def max1(i, b, us):
                for u in us:
                    if u == 0:
                        dve.wait_ge(n1_full.sem, n1_full.at(b - 1))
                    dve.wait_ge(m1_full.sem, m1_full.at(b, u + 1))
                    v.tensor_reduce(NM1[:, 2 * u:2 * u + 2],
                                    PM[maxima.slot(("B", u))][:, :].rearrange("p (a k) -> p a k", a=2), axis=AX.X,
                                    op=ALU.max, negate=True).then_inc(max_done, 1)

            def split0(i, b):
                for mt in range(2):
                    dve.wait_ge(qf_done.sem, qf_done.at(b, mt + 1))
                    dve.wait_ge(stack0_in[mt].sem, stack0_in[mt].at(b - 1))
                    v.tensor_tensor(QLO[:, mt, :], PX[other.slot(("p0", mt))][:, :], QHI[:, mt, :].bitcast(F32),
                                    ALU.subtract).then_inc(taken(("p0", mt)), 1)

            def context0(i, b, q):
                dve.wait_ge(pv_done, probs.nth(("AB"[q], 3), i))
                dve.wait_ge(cinv_done.sem, cinv_done.at(b))
                dve.wait_ge(rc_done.sem, rc_done.at(b, q))
                dve.wait_ge(tq_full.sem, tq_full.at(b - 1))
                v.tensor_tensor(R0, PD[:, :], CINV, ALU.add).then_inc(dd_done.sem, 1)
                dve.wait_ge(p0_full.sem, p0_full.at(b + 1))
                dve.wait_ge(taken(("mean", 0)), other.nth_of_slot(("mean", 0), i - 1))
                dve.wait_ge(w0_full.sem, w0_full.at(b - 1))
                v.tensor_scalar(XMC[:, q, :], CINV, MEAN[:, q, bass.ds(b, 1)], None, ALU.mult).then_inc(m_done.sem, 1)
                dve.wait_ge(dd_done.sem, dd_done.at(b, q + 1))
                v.reciprocal(R0, R0).then_inc(recip0_done.sem, 1)
                dve.wait_ge(rc_done.sem, rc_done.at(b, q + 1))
                dve.wait_ge(ctx_done.sem, ctx_done.at(b, q))
                v.tensor_tensor(TT, PO[:, :], R0, ALU.mult).then_inc(context_taken, 1)

            def residual0(i, b):
                dve.wait_ge(xres_in.sem, xres_in.at(b))
                for mt in range(2):
                    dve.wait_ge(w0_full.sem, w0_full.at(b, mt + 1))
                    v.tensor_tensor(X1[:, mt, :], PX[other.slot(("w0", mt))][:, :], X1[:, mt, :], ALU.add) \
                        .then_inc(taken(("w0", mt)), 1)

            def modulate(i, b):
                dve.wait_ge(v1_full.sem, v1_full.at(b - 1))
                for k in range(2):
                    dve.wait_ge(t1_full.sem, t1_full.at(b, k + 1))
                    for cc in range(2):
                        c = 2 * k + cc
                        last = v.tensor_scalar(XNT[:, c, :], PX[other.slot(("t1", k))][:, cc * N1:(cc + 1) * N1],
                                               AMOD[:, c, bass.ds(b, 1)], SMOD[:, c, bass.ds(b, 1)],
                                               ALU.mult, ALU.add)
                    last.then_inc(taken(("t1", k)), 1)

            def square_sums(i, b, t):
                dve.wait_ge(sq_done.sem, sq_done.at(b, t + 1))
                dve.wait_ge(rqk_done.sem, rqk_done.at(b - 1, t + 1))
                v.reduce_sum(SSQ[:, t, :], YSQ[:, :, :].rearrange("p a (h d) -> p (a h) d", d=DH), AX.X) \
                    .then_inc(ssq_done.sem, 1)

            def split1(i, b):
                dve.wait_ge(stack1_in.sem, stack1_in.at(b - 1))
                for k in range(4):
                    part, half = k // 2, k % 2
                    dve.wait_ge(kqhi_done.sem, kqhi_done.at(b, k + 1))
                    v.scalar_tensor_tensor(out=KQLO[:, part, 2 * half:2 * half + 2, :].rearrange("p c t -> p (c t)"),
                                           in0=PX[other.slot(("tq", k))][:, :], scalar=GQK[:, part:part + 1],
                                           in1=KQHI[:, part, 2 * half:2 * half + 2, :].rearrange("p c t -> p (c t)")
                                           .bitcast(F32),
                                           op0=ALU.mult, op1=ALU.subtract).then_inc(taken(("tq", k)), 1)

            def context1(i, b, c):
                dve.wait_ge(pv_done, probs.nth(("C", c), b + 1))
                if c == 0:
                    dve.wait_ge(w1_full.sem, w1_full.at(b - 1))
                    dve.wait_ge(context_taken, context.nth(("C", 3), b))
                else:
                    dve.wait_ge(context_taken, context.nth(("C", c - 1), b + 1))
                v.reciprocal(R1[:, :], PD[:, 0:N1]).then_inc(recip1_done.sem, 1)
                dve.wait_ge(recip1_done.sem, recip1_done.at(b, c + 1))
                v.tensor_tensor(OT[:, c, :], PO[:, 0:N1], R1[:, :], ALU.mult).then_inc(context_taken, 1)

            def residual1(i, b):
                dve.wait_ge(x1r_done.sem, x1r_done.at(b))
                dve.wait_ge(t0_full.sem, t0_full.at(b + 2))
                for t in range(2):
                    dve.wait_ge(w1_full.sem, w1_full.at(b, t + 1))
                    v.tensor_tensor(OUTT[:, t, :], PX[other.slot(("w1", t))][:, :], X1R[:, t, :], ALU.add) \
                        .then_inc(taken(("w1", t)), 1)

            def iteration(i):
                if has(i, -2):
                    context1(i, i - 2, 3)
                if has(i, 0):
                    max0("A", i, i, 1, units("A", 0))
                if has(i, 1):
                    sums_x(i, i + 1)
                if has(i, -1):
                    square_sums(i, i - 1, 0)
                if has(i, 0):
                    max0("A", i, i, 1, units("A", 1))
                if has(i, -1):
                    square_sums(i, i - 1, 1)
                if has(i, -2):
                    residual1(i, i - 2)
                if has(i, 0):
                    max0("A", i, i, 1, units("A", 2))
                if has(i, -1):
                    split1(i, i - 1)
                if has(i, 1):
                    split0(i, i + 1)
                if has(i, 0):
                    context0(i, i, 0)
                if has(i, -1):
                    max1(i, i - 1, range(16))
                if has(i, 0):
                    context0(i, i, 1)
                if has(i, 1):
                    max0("C", i, i + 1, 0, [*units("C", 0), *units("C", 1)])
                if has(i, -1):
                    context1(i, i - 1, 0)
                if has(i, 0):
                    residual0(i, i)
                if has(i, 1):
                    max0("C", i, i + 1, 0, units("C", 2))
                if has(i, -1):
                    context1(i, i - 1, 1)
                    context1(i, i - 1, 2)
                if has(i, 0):
                    modulate(i, i)

            modulation()
            pipeline(dve, iteration)

        @block.gpsimd
        def _(pool):
            g = nc.gpsimd

            def identity():
                g.memset(HALF[:, :], -0.5).then_inc(ident_set.sem, 1)
                g.memset(IDENT[:, :], 0.0).then_inc(ident_set.sem, 1)
                pool.wait_ge(ident_set.sem, 2)
                g.affine_select(out=IDENT[:, :], in_=IDENT[:, :], compare_op=ALU.not_equal, fill=1.0, base=0,
                                pattern=[[-1, P]], channel_multiplier=1).then_inc(ident_set.sem, 1)

            def mask_x(i, b):
                pool.wait_ge(xin_in.sem, xin_in.at(b))
                pool.wait_ge(cbm_in.sem, cbm_in.at(b))
                pool.wait_ge(p0_full.sem, p0_full.at(b - 1))
                pool.wait_ge(w0_full.sem, w0_full.at(b - 2))
                for c in range(2):
                    g.tensor_tensor(XMC[:, c, :], XIN[:, c, :], CBM[:, :], ALU.mult).then_inc(xm_done.sem, 1)

            def masked_out(i, b):
                count_0 = held(pool, cbr_in.at(b))
                count_1 = held(pool, tq_full.at(b - 1))
                pool.wait_ge(ident_set.sem, 3)
                pool.wait_ge(cbr_in.sem, count_0)
                pool.wait_ge(tq_full.sem, count_1)
                g.tensor_scalar(CINV, CBR[:, :], -1.0, 1.0, ALU.mult, ALU.add).then_inc(cinv_done.sem, 1)

            def context0(i, b, q):
                pool.wait_ge(recip0_done.sem, recip0_done.at(b, q + 1))
                g.tensor_tensor(R0, R0, CBR[:, :], ALU.mult).then_inc(rc_done.sem, 1)
                pool.wait_ge(context_taken, context.nth("AB"[q], i))
                pool.wait_ge(m_done.sem, m_done.at(b, q + 1))
                g.tensor_tensor(XMC[:, q, :], XMC[:, q, :], TT, ALU.add).then_inc(ctx_done.sem, 1)

            def keep_x1(i, b):
                count_0 = held(pool, other.nth_of_slot(("w1", 1), i))
                pool.wait_ge(ident_set.sem, 3)
                pool.wait_ge(taken(("w1", 1)), count_0)
                g.tensor_copy(X1R[:, :, :], X1[:, :, :]).then_inc(x1r_done.sem, 1)

            def norm(i, b):
                count_0 = held(pool, ss_done.at(b))
                count_1 = held(pool, y_done.at(b - 1))
                pool.wait_ge(ident_set.sem, 3)
                pool.wait_ge(ss_done.sem, count_0)
                pool.wait_ge(y_done.sem, count_1)
                g.tensor_scalar(SS[:, :], SS[:, :], 1.0 / DM, EPS, ALU.mult, ALU.add).then_inc(ms_done.sem, 1)
                pool.wait_ge(ms_done.sem, ms_done.at(b))
                g.tensor_tensor(RSTD[:, :], SS[:, :], HALF[:, 0:2], ALU.pow).then_inc(rstd_done.sem, 1)
                count_0 = held(pool, rstd_done.at(b))
                pool.wait_ge(ident_set.sem, 3)
                pool.wait_ge(rstd_done.sem, count_0)
                for t in range(2):
                    g.tensor_scalar(YSQ[:, t, :], X1[:, t, :], RSTD[:, t:t + 1], None, ALU.mult).then_inc(y_done.sem, 1)

            def norm_heads(i, b, t):
                pool.wait_ge(taken(("p1", 2 * t + 1)), other.nth_of_slot(("p1", 2 * t + 1), i))
                if t == 0:
                    pool.wait_ge(t1_full.sem, t1_full.at(b))
                else:
                    pool.wait_ge(ssq_done.sem, ssq_done.at(b, 1))
                sq = YSQ[:, :, :].rearrange("p a n -> p (a n)")
                g.tensor_tensor(sq, QK[:, t, :], QK[:, t, :], ALU.mult).then_inc(sq_done.sem, 1)
                count_0 = held(pool, ssq_done.at(b, t + 1))
                count_1 = held(pool, qn_done.at(b - 1, t + 1))
                pool.wait_ge(ident_set.sem, 3)
                pool.wait_ge(ssq_done.sem, count_0)
                pool.wait_ge(qn_done.sem, count_1)
                g.tensor_scalar(RQK[:, t, :], SSQ[:, t, :], 1.0 / DH, EPS, ALU.mult, ALU.add).then_inc(msq_done.sem, 1)
                pool.wait_ge(msq_done.sem, msq_done.at(b, t + 1))
                g.tensor_tensor(RQK[:, t, :], RQK[:, t, :], HALF[:, :], ALU.pow).then_inc(rqk_done.sem, 1)
                pool.wait_ge(rqk_done.sem, rqk_done.at(b, t + 1))
                heads = QK[:, t, :].rearrange("p (h d) -> p h d", d=DH)
                g.tensor_tensor(heads, heads, RQK[:, t, :].unsqueeze(2).broadcast_to([P, 2 * H1, DH]), ALU.mult) \
                    .then_inc(qn_done.sem, 1)

            def iteration(i):
                if has(i, 1):
                    mask_x(i, i + 1)
                if has(i, -1):
                    norm_heads(i, i - 1, 0)
                    norm_heads(i, i - 1, 1)
                if has(i, 0):
                    masked_out(i, i)
                    context0(i, i, 0)
                if has(i, -1):
                    keep_x1(i, i - 1)
                if has(i, 0):
                    context0(i, i, 1)
                    norm(i, i)

            identity()
            pipeline(pool, iteration)

        @block.sync
        def _(sp):
            def load_x(b):
                count_0 = held(sp, xm_done.at(b - 1))
                count_1 = held(sp, xs_done.at(b - 1))
                sp.wait_ge(ident_set.sem, 3)
                sp.wait_ge(xm_done.sem, count_0)
                sp.wait_ge(xs_done.sem, count_1)
                sp.dma_start(XIN[:, :, :], x_v[b]).then_inc(xin_in.sem, 16)
                sp.dma_start(CBM[:, :], cond[b].unsqueeze(0).partition_broadcast(P)).then_inc(cbm_in.sem, 16)

            def load_mask(b):
                count_0 = held(sp, ctx_done.at(b - 1))
                sp.wait_ge(ident_set.sem, 3)
                sp.wait_ge(ctx_done.sem, count_0)
                sp.dma_start(CBR[:, :], cond[b].unsqueeze(0).partition_broadcast(P)).then_inc(cbr_in.sem, 16)

            def load_residual(b):
                count_0 = held(sp, x1r_done.at(b - 1))
                count_1 = held(sp, y_done.at(b - 1))
                sp.wait_ge(ident_set.sem, 3)
                sp.wait_ge(x1r_done.sem, count_0)
                sp.wait_ge(y_done.sem, count_1)
                sp.dma_start(X1[:, :, :], x_v[b]).then_inc(xres_in.sem, 16)

            def stack(dst_a, dst_b, a_hi, a_lo, b_hi, b_lo, event):
                for dst, src in ((dst_a[0:32], a_hi), (dst_a[32:64], a_lo), (dst_a[64:96], a_hi),
                                 (dst_b[0:32], b_hi), (dst_b[32:64], b_hi), (dst_b[64:96], b_lo)):
                    sp.dma_start(dst.bitcast(F32), src.bitcast(F32)).then_inc(event.sem, 16)

            def stack0(b, q):
                count_0 = held(sp, qhi_done.at(b, q + 1))
                count_1 = held(sp, other.nth_of_slot(("p0", q), b - 1))
                count_2 = held(sp, s0_full.at(b - 1, 16 * (q + 1)))
                sp.wait_ge(ident_set.sem, 3)
                sp.wait_ge(qhi_done.sem, count_0)
                sp.wait_ge(taken(("p0", q)), count_1)
                sp.wait_ge(s0_full.sem, count_2)
                for hq in range(QH):
                    hi, lo = QHI[hq * DH:(hq + 1) * DH, q, :], QLO[hq * DH:(hq + 1) * DH, q, :]
                    h = q * QH + hq
                    stack(A0[:, h, :], B0[:, h, :], hi, lo, hi, lo, stack0_in[q])

            def stack1(b):
                count_0 = held(sp, kqhi_done.at(b))
                count_1 = held(sp, other.nth_of_slot(("tq", 3), b + 1))
                count_2 = held(sp, s1_full.at(b - 1))
                sp.wait_ge(ident_set.sem, 3)
                sp.wait_ge(kqhi_done.sem, count_0)
                sp.wait_ge(taken(("tq", 3)), count_1)
                sp.wait_ge(s1_full.sem, count_2)
                for hq in range(QH):
                    own = slice(hq * DH, (hq + 1) * DH)
                    stack(A1[:, hq, :, :], B1[:, hq, :, :], KQHI[own, 1, :, :], KQLO[own, 1, :, :],
                          KQHI[own, 0, :, :], KQLO[own, 0, :, :], stack1_in)

            def store(b):
                count_0 = held(sp, other.nth_of_slot(("w1", 1), b + 2))
                sp.wait_ge(ident_set.sem, 3)
                sp.wait_ge(taken(("w1", 1)), count_0)
                sp.dma_start(out_v[b], OUTT[:, :, :]).then_inc(stored.sem, 16)

            def iteration(i):
                if has(i, 1):
                    load_x(i + 1)
                if has(i, 0):
                    load_mask(i)
                if has(i, -2):
                    store(i - 2)
                if has(i, -1):
                    stack1(i - 1)
                if has(i, 1):
                    stack0(i + 1, 0)
                if has(i, 0):
                    load_residual(i)
                if has(i, 1):
                    stack0(i + 1, 1)

            for dst, src in ((CT[:, :, :], cond_t), (WEMB, w_emb.rearrange("(c p) n -> p c n", p=P)),
                             (WQ[:, :, :], wq_t.rearrange("(c p) n -> p c n", p=P)),
                             (WO[:, :, :], wo_t.rearrange("(c p) n -> p c n", p=P)),
                             (WQKV[:, :, :], w_qkv.rearrange("(c p) n -> p c n", p=P)),
                             (WOUT[:, :, :], w_out.rearrange("(c p) n -> p c n", p=P)),
                             (BEMB[:, :], b_emb_t), (GN[:, :], g_norm_t), (GQK[:, 0:1], g_q_t), (GQK[:, 1:2], g_k_t)):
                sp.dma_start(dst, src).then_inc(weights_in.sem, 16)
            pipeline(sp, iteration)
            sp.wait_ge(stored.sem, 16 * NB)


def kernel(x, cond_2048, L0_cond_Wq, L0_cond_Wo, L1_cond_W_emb, L1_cond_b_emb, L1_cond_g_norm, L1_cond_W_qkv,
           L1_cond_g_q, L1_cond_g_k, L1_cond_W_out):
    import concourse.bacc as _bacc
    from concourse.bass_utils import run_bass_kernel_spmd as _run

    def by_partition(v, n):
        return np.ascontiguousarray(np.asarray(v).reshape(n, P).T)

    c = np.asarray(cond_2048)
    arrays = {
        "x": np.ascontiguousarray(x),
        "cond": np.ascontiguousarray(c),
        "cond_t": np.ascontiguousarray(c.reshape(NB, 4, P).transpose(2, 1, 0)),
        "wq_t": np.ascontiguousarray(np.asarray(L0_cond_Wq).T),
        "wo_t": np.ascontiguousarray(np.asarray(L0_cond_Wo).T),
        "w_emb": np.ascontiguousarray(L1_cond_W_emb),
        "b_emb_t": by_partition(L1_cond_b_emb, 8),
        "g_norm_t": by_partition(L1_cond_g_norm, 4),
        "w_qkv": np.ascontiguousarray(L1_cond_W_qkv),
        "g_q_t": np.ascontiguousarray(np.tile(np.asarray(L1_cond_g_q), QH).reshape(P, 1)),
        "g_k_t": np.ascontiguousarray(np.tile(np.asarray(L1_cond_g_k), QH).reshape(P, 1)),
        "w_out": np.ascontiguousarray(L1_cond_W_out),
    }
    nc = _bacc.Bacc("TRN2", target_bir_lowering=False, num_devices=1)
    args = [nc.dram_tensor(n, a.shape, F32, kind="ExternalInput").ap() for n, a in arrays.items()]
    args.append(nc.dram_tensor("out", (NB, D0, T0), F32, kind="ExternalOutput").ap())
    cond_resid(nc, *args)
    r = _run(nc, [arrays], core_ids=[0])
    return r.results[0]["out"]
```

```python
from contextlib import ExitStack

import numpy as np

import concourse.bass as bass
from concourse import mybir

F32 = mybir.dt.float32
F32R = mybir.dt.float32r
ALU = mybir.AluOpType
ACT = mybir.ActivationFunctionType
AX = mybir.AxisListType

NB = 16
P = 128
D0, T0 = 256, 512
N1, DM = 256, 512
DH = 32
H0, H1 = D0 // DH, DM // DH
QH = 4
Q0, Q1 = H0 // QH, H1 // QH
KB0, KB1 = T0 // P, N1 // P
SCALE = float(DH) ** -0.5
SCALE_RAW = SCALE * DH
EPS = 1e-6
NEG = 1e30

MAX_IN = {"A": (6, 5, 5, 0), "B": (0, 4, 6, 6), "C": (6, 2, 4, 4)}


LOOP = (3, NB - 1)


def units(seg, g, k):
    first, n = sum(MAX_IN[seg][:g]), MAX_IN[seg][g]
    return range(first + k * n // QH, first + (k + 1) * n // QH)


class Event:

    def __init__(self, sem, per):
        self.sem, self.per = sem, per

    def at(self, b, n=None):
        n = self.per if n is None else n
        if not isinstance(b, int):
            return b * self.per + n
        return max(0, min(b * self.per + n, NB * self.per))


class Turns:

    def __init__(self, n, uses):
        self.n, self.uses = n, uses
        self.place = {key: k for k, (key, _) in enumerate(uses)}

    def slot(self, key):
        return self.place[key] % self.n

    def _count(self, key, i, mine):
        def upto(i):
            n = 0
            for j in range(-1, i + 1):
                for k, (_, off) in enumerate(self.uses):
                    if (j < i or k <= self.place[key]) and 0 <= j + off < NB and mine(k):
                        n += 1
            return n
        if isinstance(i, int):
            return upto(i)
        per = upto(LOOP[0] + 1) - upto(LOOP[0])
        return i * per + (upto(LOOP[0]) - LOOP[0] * per)

    def nth(self, key, i):
        return self._count(key, i, lambda k: True)

    def nth_of_slot(self, key, i):
        return self._count(key, i, lambda k: k % self.n == self.slot(key))


def before(count, n):
    return max(0, count - n) if isinstance(count, int) else count - n


def cond_resid(nc, x, cond, cond_t, wq_t, wo_t, w_emb, b_emb_t, g_norm_t, w_qkv, g_q_t, g_k_t, w_out, out):
    x_v = x.rearrange("b (c p) t -> b p c t", p=P)
    out_v = out.rearrange("b (c p) t -> b p c t", p=P)
    ctx = ExitStack()
    with ctx:
        def sb(name, shape, dt=F32):
            return ctx.enter_context(nc.sbuf_tensor(name, shape, dt))

        def pb(name, shape):
            return ctx.enter_context(nc.psum_tensor(name, shape, F32))

        def ev(name, per):
            return Event(ctx.enter_context(nc.semaphore(name)), per)

        WQ = sb("WQ", [P, 2, D0])
        WO = sb("WO", [P, 2, D0])
        WQKV = sb("WQKV", [P, 4, 3 * DM])
        WOUT = sb("WOUT", [P, 4, DM])
        CT = sb("CT", [P, 4, NB])
        KBIAS = sb("KBIAS", [P, 4, NB])
        KCOL = sb("KCOL", [P, 4])
        BEMB = sb("BEMB", [P, 8])
        GN = sb("GN", [P, 4])
        GQK = sb("GQK", [P, 2])
        AMOD = sb("AMOD", [P, 4, NB])
        SMOD = sb("SMOD", [P, 4, NB])
        IDENT = sb("IDENT", [P, P])
        ONES = sb("ONES", [P, DH])
        A0 = sb("A0", [P, H0, T0], F32R)
        B0 = sb("B0", [P, H0, T0], F32R)
        XIN = sb("XIN", [P, 2, T0])
        CBM = sb("CBM", [P, T0])
        CBR = sb("CBR", [P, T0])
        XMC = sb("XMC", [P, 2, T0])
        XS = sb("XS", [P, 2])
        MEAN = sb("MEAN", [P, 2, NB])
        QHI = sb("QHI", [P, 2, T0], F32R)
        QLO = sb("QLO", [P, 2, T0], F32R)
        QF = sb("QF", [P, 2, T0])
        OUTT = QF
        V0 = sb("V0", [P, 2, KB0, P])
        NM0 = sb("NM0", [P, 2, 16])
        NMT0 = sb("NMT0", [16, 2, P], F32R)
        A1 = sb("A1", [P, QH, Q1, N1], F32R)
        B1 = sb("B1", [P, QH, Q1, N1], F32R)
        X1 = sb("X1", [P, 2, DM])
        X1R = sb("X1R", [P, 2, DM])
        SS = sb("SS", [P, 2])
        RSTD = sb("RSTD", [P, 2])
        YSQ = sb("YSQ", [P, 2, DM])
        XNT = sb("XNT", [P, 4, N1])
        QK = sb("QK", [P, 2, 2 * DM])
        SSQ = sb("SSQ", [P, 2, 2 * H1])
        RQK = sb("RQK", [P, 2, 2 * H1])
        HALF = sb("HALF", [P, 2 * H1])
        KQHI = sb("KQHI", [P, 2, Q1, N1], F32R)
        KQLO = sb("KQLO", [P, 2, Q1, N1], F32R)
        V1 = sb("V1", [P, 2, DM])
        NM1 = sb("NM1", [P, 2 * H1])
        NMT1 = sb("NMT1", [2 * H1, P], F32R)
        R1 = sb("R1", [P, N1])
        OT = sb("OT", [P, Q1, N1])
        E = sb("E", [P, 2, QH, T0])
        WEMB = E[:, :, :, :].rearrange("p a h t -> p (a h t)").rearrange("p (c n) -> p c n", c=4)
        R0 = QK[:, 0, 0:T0]
        TT = QK[:, 0, T0:2 * T0]
        CINV = QK[:, 1, 0:T0]

        PM = [pb(f"PM{k}", [P, 512]) for k in range(2)]
        PS = [pb(f"PS{k}", [P, 512]) for k in range(2)]
        PO = pb("PO", [P, 512])
        PD = pb("PD", [P, 512])
        PX = [pb(f"PX{k}", [P, 512]) for k in range(2)]

        wq_in = ev("wq_in", 0)
        mod_in = ev("mod_in", 0)
        weights_in = ev("weights_in", 0)
        consts_set = ev("consts_set", 0)
        ident_set = ev("ident_set", 0)
        mod_full = ev("mod_full", 0)
        mod_done = ev("mod_done", 0)
        xin_in = ev("xin_in", 16)
        cbm_in = ev("cbm_in", 16)
        cbr_in = ev("cbr_in", 16)
        xres_in = ev("xres_in", 16)
        xm_done = ev("xm_done", 2)
        xs_done = ev("xs_done", 1)
        p0_full = ev("p0_full", 3)
        qhi_done = ev("qhi_done", 2)
        qf_done = ev("qf_done", 2)
        stack0_in = [[ev(f"stack0_in{q}{h}", 6 * 16) for h in range(QH)] for q in range(Q0)]
        t0_full = ev("t0_full", 2)
        m0_full = ev("m0_full", 32)
        n0_full = ev("n0_full", 2)
        row0_in = [ev(f"row0_in{q}", 16) for q in range(Q0)]
        s0_full = ev("s0_full", 32)
        kcol_done = ev("kcol_done", 1)
        cinv_done = ev("cinv_done", 1)
        recip0_done = ev("recip0_done", 4)
        rc_done = ev("rc_done", 2)
        tt_done = ev("tt_done", 2)
        m_done = ev("m_done", 2)
        ctx_done = ev("ctx_done", 2)
        w0_full = ev("w0_full", 2)
        ss_done = ev("ss_done", 2)
        ms_done = ev("ms_done", 1)
        rstd_done = ev("rstd_done", 1)
        y_done = ev("y_done", 2)
        x1r_done = ev("x1r_done", 1)
        t1_full = ev("t1_full", 2)
        p1_full = ev("p1_full", 4)
        v1_full = ev("v1_full", 2)
        sq_done = ev("sq_done", 2)
        ssq_done = ev("ssq_done", 2)
        msq_done = ev("msq_done", 2)
        rqk_done = ev("rqk_done", 2)
        qn_done = ev("qn_done", 2)
        tq_full = ev("tq_full", 4)
        kqhi_done = ev("kqhi_done", 4)
        stack1_in = [ev(f"stack1_in{h}", 6 * 16) for h in range(QH)]
        m1_full = ev("m1_full", 16)
        n1_full = ev("n1_full", 1)
        row1_in = ev("row1_in", 16)
        s1_full = ev("s1_full", 16)
        ot_done = ev("ot_done", 4)
        w1_full = ev("w1_full", 2)
        stored = ev("stored", 16)
        max_done = ctx.enter_context(nc.semaphore("max_done"))
        exp_done = ctx.enter_context(nc.semaphore("exp_done"))
        pv_done = ctx.enter_context(nc.semaphore("pv_done"))
        sum_done = ctx.enter_context(nc.semaphore("sum_done"))
        context_taken = ctx.enter_context(nc.semaphore("context_taken"))
        sums_taken = ctx.enter_context(nc.semaphore("sums_taken"))
        other_taken = [ctx.enter_context(nc.semaphore(f"other_taken{k}")) for k in range(2)]

        maxima = Turns(2, [(("A", u), 0) for u in range(16)] + [(("B", u), -1) for u in range(16)]
                       + [(("C", u), 1) for u in range(16)])
        scores = Turns(2, [(("A", u), 0) for u in range(16)] + [(("B", u), 0) for u in range(16)]
                       + [(("C", u), -1) for u in range(16)])
        probs = Turns(2, [(("A", g), 0) for g in range(4)] + [(("B", g), 0) for g in range(4)]
                      + [(("C", g), -1) for g in range(4)])
        context = Turns(1, [("A", 0), ("B", 0)] + [(("C", c), -1) for c in range(4)])
        other = Turns(2, [*[(("p1", k), -1) for k in range(4)], (("w1", 0), -2), (("w1", 1), -2), (("n0", 1), 0),
                          (("p0", 0), 1), (("p0", 1), 1), (("mean", 0), 1), *[(("tq", k), -1) for k in range(4)],
                          (("t0", 0), 1), (("n1", 0), -1), (("v1", 0), -1), (("v1", 1), -1), (("t0", 1), 1),
                          (("w0", 0), 0), (("w0", 1), 0), (("n0", 0), 1), (("t1", 0), 0), (("t1", 1), 0)])

        def has(i, off):
            return not isinstance(i, int) or 0 <= i + off < NB

        def held(eng, count):
            return count if isinstance(count, int) else eng.to_reg(count)

        def taken(key):
            return other_taken[other.slot(key)]

        def pipeline(eng, iteration, after_first):
            iteration(-1)
            after_first()
            for i in range(LOOP[0]):
                iteration(i)
            with eng.Fori(*LOOP) as i:
                iteration(i)
            for i in range(LOOP[1], NB + 2):
                iteration(i)

        block = ctx.enter_context(nc.Block())

        @block.tensor
        def _(pe):
            mm, tp = nc.tensor.matmul, nc.tensor.transpose

            def modulation():
                pe.wait_ge(mod_in.sem, 16 * 4)
                for n in range(8):
                    for c in range(4):
                        last = mm(PS[0][:, n * NB:(n + 1) * NB], WEMB[:, c, n * P:(n + 1) * P], CT[:, c, :],
                                  start=(c == 0), stop=(c == 3))
                last.then_inc(mod_full.sem, 1)
                pe.wait_ge(mod_done.sem, 1)
                pe.wait_ge(weights_in.sem, 16 * 5)
                pe.wait_ge(consts_set.sem, 4)

            def project0(i, b, mt):
                if mt == 0:
                    pe.wait_ge(xm_done.sem, xm_done.at(b))
                pe.wait_ge(taken(("p0", mt)), before(other.nth_of_slot(("p0", mt), i), 1))
                bank = PX[other.slot(("p0", mt))]
                for c in range(2):
                    last = mm(bank[:, :], WQ[:, c, mt * P:(mt + 1) * P], XMC[:, c, :], start=(c == 0), stop=(c == 1))
                last.then_inc(p0_full.sem, 1)

            def project_mean(i, b):
                pe.wait_ge(taken(("mean", 0)), before(other.nth_of_slot(("mean", 0), i), 1))
                pe.wait_ge(xs_done.sem, xs_done.at(b))
                bank = PX[other.slot(("mean", 0))]
                for mt in range(2):
                    for c in range(2):
                        last = mm(bank[:, mt:mt + 1], WQ[:, c, mt * P:(mt + 1) * P], XS[:, c:c + 1],
                                  start=(c == 0), stop=(c == 1))
                last.then_inc(p0_full.sem, 1)

            def values0(i, b, mt):
                pe.wait_ge(taken(("t0", mt)), before(other.nth_of_slot(("t0", mt), i), 1))
                pe.wait_ge(qf_done.sem, qf_done.at(b, mt + 1))
                bank = PX[other.slot(("t0", mt))]
                for kb in range(KB0):
                    last = tp(bank[:, kb * P:(kb + 1) * P], QF[:, mt, kb * P:(kb + 1) * P], IDENT[:, :])
                last.then_inc(t0_full.sem, 1)

            def max0(seg, i, b, q, u):
                hq, kb = u // KB0, u % KB0
                h = q * QH + hq
                if kb == 0:
                    pe.wait_ge(stack0_in[q][hq].sem, stack0_in[q][hq].at(b))
                pe.wait_ge(max_done, before(maxima.nth((seg, u), i), 2))
                mm(PM[maxima.slot((seg, u))][:, :], A0[0:96, h, kb * P:(kb + 1) * P], B0[0:96, h, :],
                   start=True, stop=True).then_inc(m0_full.sem, 1)

            def max1(i, b, u):
                hq, c = u // Q1, u % Q1
                if c == 0:
                    pe.wait_ge(stack1_in[hq].sem, stack1_in[hq].at(b))
                pe.wait_ge(max_done, before(maxima.nth(("B", u), i), 2))
                bank = PM[maxima.slot(("B", u))]
                for qb in range(2):
                    last = mm(bank[:, qb * N1:(qb + 1) * N1], B1[0:96, hq, c, qb * P:(qb + 1) * P], A1[0:96, hq, c, :],
                              start=True, stop=True)
                last.then_inc(m1_full.sem, 1)

            def rows0(i, b, q):
                pe.wait_ge(taken(("n0", q)), before(other.nth_of_slot(("n0", q), i), 1))
                pe.wait_ge(max_done, maxima.nth(("AC"[q == 0], 15), i))
                tp(PX[other.slot(("n0", q))][0:16, 0:P], NM0[:, q, :], IDENT[:, :]).then_inc(n0_full.sem, 1)

            def rows1(i, b):
                pe.wait_ge(taken(("n1", 0)), before(other.nth_of_slot(("n1", 0), i), 1))
                pe.wait_ge(max_done, maxima.nth(("B", 15), i))
                tp(PX[other.slot(("n1", 0))][0:2 * H1, 0:P], NM1[:, :], IDENT[:, :]).then_inc(n1_full.sem, 1)

            def score0(seg, i, b, q, g, hq):
                u, h = g * QH + hq, q * QH + hq
                if g == 0:
                    pe.wait_ge(stack0_in[q][hq].sem, stack0_in[q][hq].at(b))
                if u == 0:
                    pe.wait_ge(row0_in[q].sem, row0_in[q].at(b))
                pe.wait_ge(exp_done, before(scores.nth((seg, u), i), 2))
                mm(PS[scores.slot((seg, u))][:, :], A0[0:97, h, g * P:(g + 1) * P], B0[0:97, h, :],
                   start=True, stop=True).then_inc(s0_full.sem, 1)

            def score1(i, b, c, hq):
                u = c * QH + hq
                if u == 0:
                    pe.wait_ge(row1_in.sem, row1_in.at(b))
                pe.wait_ge(exp_done, before(scores.nth(("C", u), i), 2))
                bank = PS[scores.slot(("C", u))]
                for kb in range(KB1):
                    last = mm(bank[:, kb * N1:(kb + 1) * N1], A1[0:97, hq, c, kb * P:(kb + 1) * P], B1[0:97, hq, c, :],
                              start=True, stop=True)
                last.then_inc(s1_full.sem, 1)

            def values_weighted0(seg, i, q, g):
                if g == 0:
                    pe.wait_ge(context_taken, before(context.nth(seg, i), 1))
                    pe.wait_ge(taken(("t0", q)), other.nth_of_slot(("t0", q), i - 1))
                pe.wait_ge(exp_done, scores.nth((seg, QH * g + QH - 1), i))
                for h in range(QH):
                    last = mm(PO[h * DH:(h + 1) * DH, :], V0[:, q, g, h * DH:(h + 1) * DH],
                              E[:, probs.slot((seg, g)), h, :], start=(g == 0), stop=(g == KB0 - 1))
                last.then_inc(pv_done, 1)

            def weights_summed0(seg, i, g):
                if g == 0:
                    pe.wait_ge(sums_taken, before(context.nth(seg, i), 1))
                for h in range(QH):
                    last = mm(PD[h * DH:(h + 1) * DH, :], ONES[:, :], E[:, probs.slot((seg, g)), h, :],
                              start=(g == 0), stop=(g == KB0 - 1))
                last.then_inc(sum_done, 1)

            def values_weighted1(i, c):
                pe.wait_ge(context_taken, before(context.nth(("C", c), i), 1))
                if c == 0:
                    pe.wait_ge(taken(("v1", 0)), other.nth_of_slot(("v1", 0), i))
                    pe.wait_ge(taken(("v1", 1)), other.nth_of_slot(("v1", 1), i))
                pe.wait_ge(exp_done, scores.nth(("C", QH * c + QH - 1), i))
                for kb in range(KB1):
                    for h in range(QH):
                        last = mm(PO[h * DH:(h + 1) * DH, 0:N1], V1[:, kb, c * P + h * DH:c * P + (h + 1) * DH],
                                  E[:, probs.slot(("C", c)), h, kb * N1:(kb + 1) * N1],
                                  start=(kb == 0), stop=(kb == KB1 - 1))
                last.then_inc(pv_done, 1)

            def weights_summed1(i, c):
                pe.wait_ge(sums_taken, before(context.nth(("C", c), i), 1))
                for kb in range(KB1):
                    for h in range(QH):
                        last = mm(PD[h * DH:(h + 1) * DH, 0:N1], ONES[:, :],
                                  E[:, probs.slot(("C", c)), h, kb * N1:(kb + 1) * N1],
                                  start=(kb == 0), stop=(kb == KB1 - 1))
                last.then_inc(sum_done, 1)

            def out0(i, b, mt):
                pe.wait_ge(ctx_done.sem, ctx_done.at(b))
                pe.wait_ge(taken(("w0", mt)), before(other.nth_of_slot(("w0", mt), i), 1))
                bank = PX[other.slot(("w0", mt))]
                for c in range(2):
                    last = mm(bank[:, :], WO[:, c, mt * P:(mt + 1) * P], XMC[:, c, :], start=(c == 0), stop=(c == 1))
                last.then_inc(w0_full.sem, 1)

            def norm_rows(i, b):
                pe.wait_ge(y_done.sem, y_done.at(b))
                for k in range(2):
                    pe.wait_ge(taken(("t1", k)), before(other.nth_of_slot(("t1", k), i), 1))
                    bank = PX[other.slot(("t1", k))]
                    for cc in range(2):
                        for t in range(2):
                            c = 2 * k + cc
                            last = tp(bank[:, (2 * cc + t) * P:(2 * cc + t + 1) * P], YSQ[:, t, c * P:(c + 1) * P],
                                      IDENT[:, :])
                    last.then_inc(t1_full.sem, 1)

            def project1(i, b, key, t, part, event):
                pe.wait_ge(taken(key), before(other.nth_of_slot(key, i), 1))
                if key == ("p1", 0):
                    pe.wait_ge(taken(("t1", 1)), other.nth_of_slot(("t1", 1), i - 1))
                bank = PX[other.slot(key)]
                for c in range(4):
                    last = mm(bank[:, :], XNT[:, c, t * P:(t + 1) * P], WQKV[:, c, part * DM:(part + 1) * DM],
                              start=(c == 0), stop=(c == 3))
                last.then_inc(event.sem, 1)

            def heads_rows(i, b, part):
                pe.wait_ge(qn_done.sem, qn_done.at(b))
                for k in range(2):
                    key = ("tq", 2 * part + k)
                    pe.wait_ge(taken(key), before(other.nth_of_slot(key, i), 1))
                    bank = PX[other.slot(key)]
                    for cc in range(2):
                        for t in range(2):
                            c = 2 * k + cc
                            last = tp(bank[:, (2 * cc + t) * P:(2 * cc + t + 1) * P],
                                      QK[:, t, part * DM + c * P:part * DM + (c + 1) * P], IDENT[:, :])
                    last.then_inc(tq_full.sem, 1)

            def out1(i, b, t):
                pe.wait_ge(ot_done.sem, ot_done.at(b))
                pe.wait_ge(taken(("w1", t)), before(other.nth_of_slot(("w1", t), i), 1))
                bank = PX[other.slot(("w1", t))]
                for c in range(4):
                    last = mm(bank[:, :], OT[:, c, t * P:(t + 1) * P], WOUT[:, c, :], start=(c == 0), stop=(c == 3))
                last.then_inc(w1_full.sem, 1)

            def iteration(i):
                def step_a(g, k):
                    if has(i, 0):
                        score0("A", i, i, 0, g, k)
                        for u in units("A", g, k):
                            max0("A", i, i, 1, u)

                def step_b(g, k):
                    if has(i, 0):
                        score0("B", i, i, 1, g, k)
                    if has(i, -1):
                        for u in units("B", g, k):
                            max1(i, i - 1, u)

                def step_c(g, k):
                    if has(i, -1):
                        score1(i, i - 1, g, k)
                    if has(i, 1):
                        for u in units("C", g, k):
                            max0("C", i, i + 1, 0, u)

                step_a(0, 0)
                if has(i, -2):
                    values_weighted1(i - 1, 3)
                step_a(0, 1)
                if has(i, -2):
                    weights_summed1(i - 1, 3)
                step_a(0, 2)
                if has(i, -1):
                    project1(i, i - 1, ("p1", 0), 0, 0, p1_full)
                step_a(0, 3)
                if has(i, -1):
                    project1(i, i - 1, ("p1", 1), 0, 1, p1_full)
                step_a(1, 0)
                if has(i, 0):
                    values_weighted0("A", i, 0, 0)
                step_a(1, 1)
                if has(i, -1):
                    project1(i, i - 1, ("p1", 2), 1, 0, p1_full)
                step_a(1, 2)
                if has(i, 0):
                    weights_summed0("A", i, 0)
                step_a(1, 3)
                if has(i, -1):
                    project1(i, i - 1, ("p1", 3), 1, 1, p1_full)
                step_a(2, 0)
                if has(i, 0):
                    values_weighted0("A", i, 0, 1)
                step_a(2, 1)
                if has(i, -2):
                    out1(i, i - 2, 0)
                step_a(2, 2)
                if has(i, 0):
                    weights_summed0("A", i, 1)
                step_a(2, 3)
                if has(i, -2):
                    out1(i, i - 2, 1)
                step_a(3, 0)
                if has(i, 0):
                    rows0(i, i, 1)
                step_a(3, 1)
                if has(i, 0):
                    values_weighted0("A", i, 0, 2)
                if has(i, 1):
                    project0(i, i + 1, 0)
                step_a(3, 2)
                if has(i, 0):
                    weights_summed0("A", i, 2)
                step_a(3, 3)
                if has(i, 1):
                    project0(i, i + 1, 1)
                    project_mean(i, i + 1)

                step_b(0, 0)
                if has(i, -1):
                    heads_rows(i, i - 1, 0)
                step_b(0, 1)
                if has(i, 0):
                    values_weighted0("A", i, 0, 3)
                step_b(0, 2)
                if has(i, -1):
                    heads_rows(i, i - 1, 1)
                step_b(0, 3)
                if has(i, 0):
                    weights_summed0("A", i, 3)
                step_b(1, 0)
                if has(i, 1):
                    values0(i, i + 1, 0)
                for g in range(1, 4):
                    if g > 1:
                        step_b(g, 0)
                    step_b(g, 1)
                    if has(i, 0):
                        values_weighted0("B", i, 1, g - 1)
                    step_b(g, 2)
                    step_b(g, 3)
                    if has(i, 0):
                        weights_summed0("B", i, g - 1)
                if has(i, -1):
                    rows1(i, i - 1)
                    project1(i, i - 1, ("v1", 0), 0, 2, v1_full)

                step_c(0, 0)
                step_c(0, 1)
                if has(i, 0):
                    values_weighted0("B", i, 1, 3)
                step_c(0, 2)
                if has(i, -1):
                    project1(i, i - 1, ("v1", 1), 1, 2, v1_full)
                step_c(0, 3)
                if has(i, 0):
                    weights_summed0("B", i, 3)
                step_c(1, 0)
                if has(i, 1):
                    values0(i, i + 1, 1)
                for g in range(1, 4):
                    if g > 1:
                        step_c(g, 0)
                    step_c(g, 1)
                    if has(i, -1):
                        values_weighted1(i, g - 1)
                    step_c(g, 2)
                    step_c(g, 3)
                    if has(i, -1):
                        weights_summed1(i, g - 1)
                    if g == 2 and has(i, 0):
                        out0(i, i, 0)
                        out0(i, i, 1)
                if has(i, 1):
                    rows0(i, i + 1, 0)
                if has(i, 0):
                    norm_rows(i, i)

            pe.wait_ge(wq_in.sem, 16)
            pe.wait_ge(ident_set.sem, 3)
            pipeline(pe, iteration, modulation)

        @block.scalar
        def _(act):
            fn = nc.scalar.activation

            def copy(o, i_):
                return fn(o, i_, ACT.Copy)

            def key_bias(i, b):
                count_0 = held(act, scores.nth(("B", 15), i - 1))
                act.wait_ge(ident_set.sem, 3)
                act.wait_ge(exp_done, count_0)
                copy(KCOL[:, :].unsqueeze(2), KBIAS[:, :, bass.ds(b, 1)]).then_inc(kcol_done.sem, 1)
                act.wait_ge(kcol_done.sem, kcol_done.at(b))

            def exp0(seg, i, b, q, g, h):
                if h == 0:
                    act.wait_ge(sum_done, before(probs.nth((seg, g), i), 2))
                u = g * QH + h
                act.wait_ge(s0_full.sem, s0_full.at(b, 16 * q + u + 1))
                fn(E[:, probs.slot((seg, g)), h, :], PS[scores.slot((seg, u))][:, :], ACT.Exp,
                   bias=KCOL[:, g:g + 1], scale=SCALE).then_inc(exp_done, 1)

            def exp1(i, b, c, h):
                if h == 0:
                    act.wait_ge(sum_done, before(probs.nth(("C", c), i), 2))
                u = c * QH + h
                act.wait_ge(s1_full.sem, s1_full.at(b, u + 1))
                fn(E[:, probs.slot(("C", c)), h, :], PS[scores.slot(("C", u))][:, :], ACT.Exp,
                   scale=SCALE_RAW).then_inc(exp_done, 1)

            def take_context0(seg, i, b, q):
                act.wait_ge(pv_done, probs.nth((seg, 3), i))
                act.wait_ge(tq_full.sem, tq_full.at(b - 1))
                act.wait_ge(ctx_done.sem, ctx_done.at(b, q))
                copy(TT, PO[:, :]).then_inc(context_taken, 1)

            def take_context1(i, b, c):
                act.wait_ge(pv_done, probs.nth(("C", c), i))
                if c == 0:
                    act.wait_ge(w1_full.sem, w1_full.at(b - 1))
                copy(OT[:, c, :], PO[:, 0:N1]).then_inc(context_taken, 1)

            def split0(i, b, mt):
                bank = PX[other.slot(("p0", mt))]
                act.wait_ge(p0_full.sem, p0_full.at(b, mt + 1))
                for h in range(QH):
                    act.wait_ge(stack0_in[mt][h].sem, stack0_in[mt][h].at(b - 1))
                copy(QHI[:, mt, :], bank[:, :]).then_inc(qhi_done.sem, 1)
                act.wait_ge(t0_full.sem, t0_full.at(b - 1, mt + 1))
                act.wait_ge(stored.sem, stored.at(b - 3))
                copy(QF[:, mt, :], bank[:, :]).then_inc(qf_done.sem, 1)

            def mean0(i, b):
                count_0 = held(act, p0_full.at(b, 3))
                act.wait_ge(ident_set.sem, 3)
                act.wait_ge(p0_full.sem, count_0)
                fn(MEAN[:, :, bass.ds(b, 1)], PX[other.slot(("mean", 0))][:, 0:2].rearrange("p (a o) -> p a o", o=1),
                   ACT.Copy, scale=1.0 / T0).then_inc(taken(("mean", 0)), 1)

            def values0(i, b, mt):
                act.wait_ge(t0_full.sem, t0_full.at(b, mt + 1))
                act.wait_ge(pv_done, probs.nth(("AB"[mt], 3), i))
                copy(V0[:, mt, :, :], PX[other.slot(("t0", mt))][:, :].rearrange("p (k d) -> p k d", k=KB0)) \
                    .then_inc(taken(("t0", mt)), 1)

            def rows0(i, b, q):
                act.wait_ge(n0_full.sem, n0_full.at(b, 1 if q == 0 else 2))
                act.wait_ge(row0_in[q].sem, row0_in[q].at(b - 1))
                copy(NMT0[:, q, :], PX[other.slot(("n0", q))][0:16, 0:P]).then_inc(taken(("n0", q)), 1)
                act.wait_ge(taken(("n0", q)), other.nth_of_slot(("n0", q), i))
                act.dma_start(B0[96:97, q * QH:(q + 1) * QH, :].rearrange("p h (k t) -> p (h k) t", t=P).bitcast(F32),
                              NMT0[:, q, :].bitcast(F32)).then_inc(row0_in[q].sem, 16)

            def rows1(i, b):
                act.wait_ge(n1_full.sem, n1_full.at(b))
                act.wait_ge(row1_in.sem, row1_in.at(b - 1))
                copy(NMT1[:, :], PX[other.slot(("n1", 0))][0:2 * H1, 0:P]).then_inc(taken(("n1", 0)), 1)
                act.wait_ge(taken(("n1", 0)), other.nth_of_slot(("n1", 0), i))
                act.dma_start(B1[96:97, :, :, :].rearrange("p h c (k t) -> p (h c k) t", t=P).bitcast(F32),
                              NMT1[:, :].bitcast(F32)).then_inc(row1_in.sem, 16)

            def heads(i, b, k):
                act.wait_ge(p1_full.sem, p1_full.at(b, k + 1))
                if k % 2 == 0:
                    act.wait_ge(ctx_done.sem, ctx_done.at(b))
                    act.wait_ge(qn_done.sem, qn_done.at(b - 1, k // 2 + 1))
                if k == 0:
                    act.wait_ge(tq_full.sem, tq_full.at(b - 1))
                copy(QK[:, k // 2, (k % 2) * DM:(k % 2 + 1) * DM], PX[other.slot(("p1", k))][:, :]) \
                    .then_inc(taken(("p1", k)), 1)

            def values1(i, b, t):
                act.wait_ge(v1_full.sem, v1_full.at(b, t + 1))
                act.wait_ge(pv_done, probs.nth(("C", 3), i - 1))
                copy(V1[:, t, :], PX[other.slot(("v1", t))][:, :]).then_inc(taken(("v1", t)), 1)

            def split1(i, b, part):
                for k in (2 * part, 2 * part + 1):
                    act.wait_ge(tq_full.sem, tq_full.at(b, k + 1))
                    if k == 0:
                        for h in range(QH):
                            act.wait_ge(stack1_in[h].sem, stack1_in[h].at(b - 1))
                    fn(KQHI[:, part, 2 * (k % 2):2 * (k % 2) + 2, :],
                       PX[other.slot(("tq", k))][:, :].rearrange("p (c t) -> p c t", c=2),
                       ACT.Copy, scale=GQK[:, part:part + 1]).then_inc(kqhi_done.sem, 1)

            def squares(i, b, t):
                if t == 0:
                    act.wait_ge(ssq_done.sem, ssq_done.at(b - 1))
                    act.wait_ge(t1_full.sem, t1_full.at(b - 1))
                    act.wait_ge(rstd_done.sem, rstd_done.at(b - 1))
                act.wait_ge(taken(("w0", t)), other.nth_of_slot(("w0", t), i))
                fn(YSQ[:, t, :], X1[:, t, :], ACT.Square, accum_out=SS[:, t:t + 1]).then_inc(ss_done.sem, 1)

            def norm(i, b):
                act.wait_ge(rstd_done.sem, rstd_done.at(b))
                for t in range(2):
                    fn(YSQ[:, t, :], X1[:, t, :], ACT.Copy, scale=RSTD[:, t:t + 1]).then_inc(y_done.sem, 1)

            def iteration(i):
                def step_a(g, *heads_):
                    if has(i, 0):
                        for h in heads_:
                            exp0("A", i, i, 0, g, h)

                def step_b(g, *heads_):
                    if has(i, 0):
                        for h in heads_:
                            exp0("B", i, i, 1, g, h)

                def step_c(g, *heads_):
                    if has(i, -1):
                        for h in heads_:
                            exp1(i, i - 1, g, h)

                if has(i, 0):
                    key_bias(i, i)
                step_a(0, 0)
                if has(i, -2):
                    take_context1(i - 1, i - 2, 3)
                step_a(0, 1, 2)
                if has(i, -1):
                    heads(i, i - 1, 0)
                step_a(0, 3)
                if has(i, -1):
                    heads(i, i - 1, 1)
                step_a(1, 0, 1)
                if has(i, -1):
                    heads(i, i - 1, 2)
                step_a(1, 2, 3)
                if has(i, -1):
                    heads(i, i - 1, 3)
                step_a(2, 0, 1, 2, 3)
                step_a(3, 0)
                if has(i, 0):
                    rows0(i, i, 1)
                step_a(3, 1)
                if has(i, 1):
                    split0(i, i + 1, 0)
                step_a(3, 2, 3)
                if has(i, 1):
                    split0(i, i + 1, 1)
                    mean0(i, i + 1)
                step_b(0, 0)
                if has(i, -1):
                    split1(i, i - 1, 0)
                step_b(0, 1, 2)
                if has(i, -1):
                    split1(i, i - 1, 1)
                if has(i, 0):
                    take_context0("A", i, i, 0)
                step_b(0, 3)
                step_b(1, 0)
                if has(i, 1):
                    values0(i, i + 1, 0)
                step_b(1, 1, 2, 3)
                step_b(2, 0, 1, 2, 3)
                step_b(3, 0, 1, 2, 3)
                if has(i, -1):
                    rows1(i, i - 1)
                    values1(i, i - 1, 0)
                step_c(0, 0, 1)
                if has(i, 0):
                    take_context0("B", i, i, 1)
                step_c(0, 2)
                if has(i, -1):
                    values1(i, i - 1, 1)
                step_c(0, 3)
                step_c(1, 0)
                if has(i, 1):
                    values0(i, i + 1, 1)
                step_c(1, 1)
                if has(i, -1):
                    take_context1(i, i - 1, 0)
                step_c(1, 2, 3)
                step_c(2, 0, 1)
                if has(i, -1):
                    take_context1(i, i - 1, 1)
                step_c(2, 2, 3)
                step_c(3, 0)
                if has(i, 0):
                    squares(i, i, 0)
                step_c(3, 1)
                if has(i, 0):
                    squares(i, i, 1)
                if has(i, -1):
                    take_context1(i, i - 1, 2)
                step_c(3, 2)
                if has(i, 0):
                    norm(i, i)
                step_c(3, 3)
                if has(i, 1):
                    rows0(i, i + 1, 0)

            def loads():
                act.wait_ge(wq_in.sem, 16)
                act.wait_ge(xin_in.sem, xin_in.at(0))
                for dst, src in ((CT[:, :, :], cond_t), (WEMB, w_emb.rearrange("(c p) n -> p c n", p=P)),
                                 (BEMB[:, :], b_emb_t), (GN[:, :], g_norm_t)):
                    act.dma_start(dst, src).then_inc(mod_in.sem, 16)
                for dst, src in ((WO[:, :, :], wo_t.rearrange("(c p) n -> p c n", p=P)),
                                 (WQKV[:, :, :], w_qkv.rearrange("(c p) n -> p c n", p=P)),
                                 (WOUT[:, :, :], w_out.rearrange("(c p) n -> p c n", p=P)),
                                 (GQK[:, 0:1], g_q_t), (GQK[:, 1:2], g_k_t)):
                    act.dma_start(dst, src).then_inc(weights_in.sem, 16)

            def modulation():
                act.wait_ge(weights_in.sem, 16 * 5)
                act.wait_ge(consts_set.sem, 4)
                act.wait_ge(mod_done.sem, 1)

            loads()
            pipeline(act, iteration, modulation)

        @block.vector
        def _(dve):
            v = nc.vector

            def constants():
                v.memset(ONES[:, :], 1.0).then_inc(consts_set.sem, 1)
                v.memset(A0[96:97, :, :].bitcast(F32), 1.0).then_inc(consts_set.sem, 1)
                v.memset(A1[96:97, :, :, :].bitcast(F32), 1.0).then_inc(consts_set.sem, 1)
                dve.wait_ge(ident_set.sem, 3)

            def modulation():
                dve.wait_ge(mod_in.sem, 16 * 4)
                dve.wait_ge(weights_in.sem, 16 * 5)
                v.tensor_scalar(KBIAS[:, :, :], CT[:, :, :], 1.0, NEG, ALU.subtract, ALU.mult).then_inc(consts_set.sem, 1)
                for c in range(4):
                    blk = WOUT[:, c, c * P:(c + 1) * P]
                    v.tensor_tensor(blk, blk, IDENT[:, :], ALU.add)
                dve.wait_ge(mod_full.sem, 1)
                for n in range(4):
                    v.tensor_scalar(AMOD[:, n, :], PS[0][:, n * NB:(n + 1) * NB], BEMB[:, n:n + 1], 1.0, ALU.add, ALU.add)
                for n in range(4):
                    last = v.tensor_scalar(SMOD[:, n, :], PS[0][:, (4 + n) * NB:(5 + n) * NB], BEMB[:, 4 + n:5 + n], None,
                                           ALU.add)
                last.then_inc(mod_done.sem, 1)
                dve.wait_ge(mod_done.sem, 1)
                for n in range(4):
                    last = v.tensor_scalar(AMOD[:, n, :], AMOD[:, n, :], GN[:, n:n + 1], float(DM) ** 0.5,
                                           ALU.mult, ALU.mult)
                last.then_inc(mod_done.sem, 1)
                dve.wait_ge(mod_done.sem, 2)

            def sums_x(i, b):
                dve.wait_ge(xin_in.sem, xin_in.at(b))
                dve.wait_ge(p0_full.sem, p0_full.at(b - 1))
                v.reduce_sum(XS[:, :], XIN[:, :, :], AX.X).then_inc(xs_done.sem, 1)

            def max0(seg, i, b, q, u):
                if u == 0:
                    dve.wait_ge(n0_full.sem, n0_full.at(b - 1, q + 1))
                dve.wait_ge(m0_full.sem, m0_full.at(b, 16 * q + u + 1))
                v.tensor_reduce(NM0[:, q, u:u + 1], PM[maxima.slot((seg, u))][:, :], axis=AX.X, op=ALU.max,
                                negate=True).then_inc(max_done, 1)

            def max1(i, b, u):
                if u == 0:
                    dve.wait_ge(n1_full.sem, n1_full.at(b - 1))
                dve.wait_ge(m1_full.sem, m1_full.at(b, u + 1))
                v.tensor_reduce(NM1[:, 2 * u:2 * u + 2],
                                PM[maxima.slot(("B", u))][:, :].rearrange("p (a k) -> p a k", a=2), axis=AX.X,
                                op=ALU.max, negate=True).then_inc(max_done, 1)

            def split0(i, b, mt):
                dve.wait_ge(qf_done.sem, qf_done.at(b, mt + 1))
                for h in range(QH):
                    dve.wait_ge(stack0_in[mt][h].sem, stack0_in[mt][h].at(b - 1))
                v.tensor_tensor(QLO[:, mt, :], PX[other.slot(("p0", mt))][:, :], QHI[:, mt, :].bitcast(F32),
                                ALU.subtract).then_inc(taken(("p0", mt)), 1)

            def take_sums0(i, b, q):
                dve.wait_ge(sum_done, probs.nth(("AB"[q], 3), i))
                dve.wait_ge(cinv_done.sem, cinv_done.at(b))
                dve.wait_ge(ctx_done.sem, ctx_done.at(b, q))
                dve.wait_ge(tq_full.sem, tq_full.at(b - 1))
                v.tensor_tensor(R0, PD[:, :], CINV, ALU.add).then_inc(sums_taken, 1)
                dve.wait_ge(p0_full.sem, p0_full.at(b + 1))
                dve.wait_ge(taken(("mean", 0)), other.nth_of_slot(("mean", 0), i - 1))
                dve.wait_ge(w0_full.sem, w0_full.at(b - 1))
                v.tensor_scalar(XMC[:, q, :], CINV, MEAN[:, q, bass.ds(b, 1)], None, ALU.mult).then_inc(m_done.sem, 1)

            def invert0(i, b, q, half):
                dve.wait_ge(sums_taken, context.nth("AB"[q], i))
                r0 = R0[:, half * (T0 // 2):(half + 1) * (T0 // 2)]
                v.reciprocal(r0, r0).then_inc(recip0_done.sem, 1)

            def residual0(i, b):
                dve.wait_ge(xres_in.sem, xres_in.at(b))
                for mt in range(2):
                    dve.wait_ge(w0_full.sem, w0_full.at(b, mt + 1))
                    v.tensor_tensor(X1[:, mt, :], PX[other.slot(("w0", mt))][:, :], X1[:, mt, :], ALU.add) \
                        .then_inc(taken(("w0", mt)), 1)

            def mean_square(i, b):
                dve.wait_ge(ss_done.sem, ss_done.at(b))
                dve.wait_ge(y_done.sem, y_done.at(b - 1))
                v.tensor_scalar(RSTD[:, :], SS[:, :], DM * EPS, None, ALU.add).then_inc(ms_done.sem, 1)

            def modulate(i, b):
                dve.wait_ge(v1_full.sem, v1_full.at(b - 1))
                for k in range(2):
                    dve.wait_ge(t1_full.sem, t1_full.at(b, k + 1))
                    for cc in range(2):
                        c = 2 * k + cc
                        last = v.tensor_scalar(XNT[:, c, :], PX[other.slot(("t1", k))][:, cc * N1:(cc + 1) * N1],
                                               AMOD[:, c, bass.ds(b, 1)], SMOD[:, c, bass.ds(b, 1)],
                                               ALU.mult, ALU.add)
                    last.then_inc(taken(("t1", k)), 1)

            def square_sums(i, b, t):
                dve.wait_ge(sq_done.sem, sq_done.at(b, t + 1))
                dve.wait_ge(msq_done.sem, msq_done.at(b - 1, t + 1))
                v.reduce_sum(SSQ[:, t, :], YSQ[:, :, :].rearrange("p a (h d) -> p (a h) d", d=DH), AX.X) \
                    .then_inc(ssq_done.sem, 1)
                dve.wait_ge(ssq_done.sem, ssq_done.at(b, t + 1))
                dve.wait_ge(qn_done.sem, qn_done.at(b - 1, t + 1))
                v.tensor_scalar(RQK[:, t, :], SSQ[:, t, :], DH * EPS, None, ALU.add).then_inc(msq_done.sem, 1)

            def split1(i, b, part):
                for k in (2 * part, 2 * part + 1):
                    dve.wait_ge(kqhi_done.sem, kqhi_done.at(b, k + 1))
                    own = slice(2 * (k % 2), 2 * (k % 2) + 2)
                    v.scalar_tensor_tensor(out=KQLO[:, part, own, :].rearrange("p c t -> p (c t)"),
                                           in0=PX[other.slot(("tq", k))][:, :], scalar=GQK[:, part:part + 1],
                                           in1=KQHI[:, part, own, :].rearrange("p c t -> p (c t)").bitcast(F32),
                                           op0=ALU.mult, op1=ALU.subtract).then_inc(taken(("tq", k)), 1)

            def context1(i, b, c):
                dve.wait_ge(sum_done, probs.nth(("C", c), i))
                dve.wait_ge(ot_done.sem, ot_done.at(b, c))
                v.reciprocal(R1[:, :], PD[:, 0:N1]).then_inc(sums_taken, 1)
                dve.wait_ge(sums_taken, context.nth(("C", c), i))
                dve.wait_ge(context_taken, context.nth(("C", c), i))
                v.tensor_tensor(OT[:, c, :], OT[:, c, :], R1[:, :], ALU.mult).then_inc(ot_done.sem, 1)

            def residual1(i, b, t):
                if t == 0:
                    dve.wait_ge(x1r_done.sem, x1r_done.at(b))
                    dve.wait_ge(t0_full.sem, t0_full.at(b + 2))
                dve.wait_ge(w1_full.sem, w1_full.at(b, t + 1))
                v.tensor_tensor(OUTT[:, t, :], PX[other.slot(("w1", t))][:, :], X1R[:, t, :], ALU.add) \
                    .then_inc(taken(("w1", t)), 1)

            def iteration(i):
                def step_a(g, *steps):
                    if has(i, 0):
                        for k in steps:
                            for u in units("A", g, k):
                                max0("A", i, i, 1, u)

                def step_b(g, *steps):
                    if has(i, -1):
                        for k in steps:
                            for u in units("B", g, k):
                                max1(i, i - 1, u)

                def step_c(g, *steps):
                    if has(i, 1):
                        for k in steps:
                            for u in units("C", g, k):
                                max0("C", i, i + 1, 0, u)

                step_a(0, 0, 1)
                if has(i, -2):
                    context1(i - 1, i - 2, 3)
                step_a(0, 2, 3)
                if has(i, 1):
                    sums_x(i, i + 1)
                step_a(1, 0, 1)
                if has(i, -1):
                    square_sums(i, i - 1, 0)
                step_a(1, 2, 3)
                step_a(2, 0, 1)
                if has(i, -1):
                    square_sums(i, i - 1, 1)
                step_a(2, 2)
                if has(i, -2):
                    residual1(i, i - 2, 0)
                step_a(2, 3)
                if has(i, -2):
                    residual1(i, i - 2, 1)
                step_a(3, 0, 1, 2, 3)
                if has(i, 1):
                    split0(i, i + 1, 0)
                    split0(i, i + 1, 1)
                if has(i, -1):
                    split1(i, i - 1, 0)
                    split1(i, i - 1, 1)
                if has(i, 0):
                    take_sums0(i, i, 0)
                step_b(1, 0)
                if has(i, 0):
                    invert0(i, i, 0, 0)
                step_b(1, 1, 2)
                if has(i, 0):
                    invert0(i, i, 0, 1)
                step_b(1, 3)
                step_b(2, 0, 1, 2, 3)
                step_b(3, 0, 1, 2, 3)
                step_c(0, 0, 1, 2, 3)
                if has(i, 0):
                    take_sums0(i, i, 1)
                    invert0(i, i, 1, 0)
                step_c(1, 0, 1)
                if has(i, 0):
                    invert0(i, i, 1, 1)
                step_c(1, 2, 3)
                if has(i, -1):
                    context1(i, i - 1, 0)
                step_c(2, 0, 1, 2, 3)
                if has(i, -1):
                    context1(i, i - 1, 1)
                if has(i, 0):
                    residual0(i, i)
                step_c(3, 0, 1)
                if has(i, 0):
                    mean_square(i, i)
                step_c(3, 2, 3)
                if has(i, -1):
                    context1(i, i - 1, 2)
                if has(i, 0):
                    modulate(i, i)

            constants()
            pipeline(dve, iteration, modulation)

        @block.gpsimd
        def _(pool):
            g = nc.gpsimd

            def identity():
                g.memset(HALF[:, :], -0.5).then_inc(ident_set.sem, 1)
                g.memset(IDENT[:, :], 0.0).then_inc(ident_set.sem, 1)
                pool.wait_ge(ident_set.sem, 2)
                g.affine_select(out=IDENT[:, :], in_=IDENT[:, :], compare_op=ALU.not_equal, fill=1.0, base=0,
                                pattern=[[-1, P]], channel_multiplier=1).then_inc(ident_set.sem, 1)

            def mask_x(i, b, c):
                pool.wait_ge(xin_in.sem, xin_in.at(b))
                pool.wait_ge(cbm_in.sem, cbm_in.at(b))
                pool.wait_ge(p0_full.sem, p0_full.at(b - 1))
                pool.wait_ge(w0_full.sem, w0_full.at(b - 2))
                g.tensor_tensor(XMC[:, c, :], XIN[:, c, :], CBM[:, :], ALU.mult).then_inc(xm_done.sem, 1)

            def masked_out(i, b):
                count_0 = held(pool, cbr_in.at(b))
                count_1 = held(pool, tq_full.at(b - 1))
                pool.wait_ge(ident_set.sem, 3)
                pool.wait_ge(cbr_in.sem, count_0)
                pool.wait_ge(tq_full.sem, count_1)
                g.tensor_scalar(CINV, CBR[:, :], -1.0, 1.0, ALU.mult, ALU.add).then_inc(cinv_done.sem, 1)

            def context0(i, b, q):
                pool.wait_ge(recip0_done.sem, recip0_done.at(b, 2 * q + 2))
                g.tensor_tensor(R0, R0, CBR[:, :], ALU.mult).then_inc(rc_done.sem, 1)
                pool.wait_ge(rc_done.sem, rc_done.at(b, q + 1))
                pool.wait_ge(context_taken, context.nth("AB"[q], i))
                g.tensor_tensor(TT, TT, R0, ALU.mult).then_inc(tt_done.sem, 1)
                pool.wait_ge(tt_done.sem, tt_done.at(b, q + 1))
                pool.wait_ge(m_done.sem, m_done.at(b, q + 1))
                g.tensor_tensor(XMC[:, q, :], XMC[:, q, :], TT, ALU.add).then_inc(ctx_done.sem, 1)

            def keep_x1(i, b):
                count_0 = held(pool, other.nth_of_slot(("w1", 1), i))
                pool.wait_ge(ident_set.sem, 3)
                pool.wait_ge(taken(("w1", 1)), count_0)
                g.tensor_copy(X1R[:, :, :], X1[:, :, :]).then_inc(x1r_done.sem, 1)

            def squares_heads(i, b, t):
                pool.wait_ge(taken(("p1", 2 * t + 1)), other.nth_of_slot(("p1", 2 * t + 1), i))
                if t == 0:
                    pool.wait_ge(t1_full.sem, t1_full.at(b))
                else:
                    pool.wait_ge(ssq_done.sem, ssq_done.at(b, 1))
                sq = YSQ[:, :, :].rearrange("p a n -> p (a n)")
                g.tensor_tensor(sq, QK[:, t, :], QK[:, t, :], ALU.mult).then_inc(sq_done.sem, 1)

            def norm_heads(i, b, t):
                pool.wait_ge(msq_done.sem, msq_done.at(b, t + 1))
                g.tensor_tensor(RQK[:, t, :], RQK[:, t, :], HALF[:, :], ALU.pow).then_inc(rqk_done.sem, 1)
                pool.wait_ge(rqk_done.sem, rqk_done.at(b, t + 1))
                heads = QK[:, t, :].rearrange("p (h d) -> p h d", d=DH)
                g.tensor_tensor(heads, heads, RQK[:, t, :].unsqueeze(2).broadcast_to([P, 2 * H1, DH]), ALU.mult) \
                    .then_inc(qn_done.sem, 1)

            def rstd(i, b):
                pool.wait_ge(ms_done.sem, ms_done.at(b))
                g.tensor_tensor(RSTD[:, :], RSTD[:, :], HALF[:, 0:2], ALU.pow).then_inc(rstd_done.sem, 1)

            def iteration(i):
                for t in range(2):
                    if has(i, -1):
                        squares_heads(i, i - 1, t)
                    if has(i, 1):
                        mask_x(i, i + 1, t)
                    if has(i, -1):
                        norm_heads(i, i - 1, t)
                if has(i, 0):
                    masked_out(i, i)
                if has(i, -1):
                    keep_x1(i, i - 1)
                if has(i, 0):
                    context0(i, i, 0)
                if has(i, 0):
                    context0(i, i, 1)
                    rstd(i, i)

            def no_modulation():
                pass

            identity()
            pipeline(pool, iteration, no_modulation)

        @block.sync
        def _(sp):
            def load_x(b):
                count_0 = held(sp, xm_done.at(b - 1))
                count_1 = held(sp, xs_done.at(b - 1))
                sp.wait_ge(ident_set.sem, 3)
                sp.wait_ge(xm_done.sem, count_0)
                sp.wait_ge(xs_done.sem, count_1)
                sp.dma_start(XIN[:, :, :], x_v[b]).then_inc(xin_in.sem, 16)
                sp.dma_start(CBM[:, :], cond[b].unsqueeze(0).partition_broadcast(P)).then_inc(cbm_in.sem, 16)

            def load_mask(b):
                count_0 = held(sp, ctx_done.at(b - 1))
                sp.wait_ge(ident_set.sem, 3)
                sp.wait_ge(ctx_done.sem, count_0)
                sp.dma_start(CBR[:, :], cond[b].unsqueeze(0).partition_broadcast(P)).then_inc(cbr_in.sem, 16)

            def load_residual(b):
                count_0 = held(sp, x1r_done.at(b - 1))
                count_1 = held(sp, y_done.at(b - 1))
                sp.wait_ge(ident_set.sem, 3)
                sp.wait_ge(x1r_done.sem, count_0)
                sp.wait_ge(y_done.sem, count_1)
                sp.dma_start(X1[:, :, :], x_v[b]).then_inc(xres_in.sem, 16)

            def stack(dst_a, dst_b, a_hi, a_lo, b_hi, b_lo, event):
                for dst, src in ((dst_a[0:32], a_hi), (dst_a[32:64], a_lo), (dst_a[64:96], a_hi),
                                 (dst_b[0:32], b_hi), (dst_b[32:64], b_hi), (dst_b[64:96], b_lo)):
                    sp.dma_start(dst.bitcast(F32), src.bitcast(F32)).then_inc(event.sem, 16)

            def stack0(b, q):
                count_0 = held(sp, qhi_done.at(b, q + 1))
                count_1 = held(sp, other.nth_of_slot(("p0", q), b - 1))
                count_2 = held(sp, s0_full.at(b - 1, 16 * (q + 1)))
                sp.wait_ge(ident_set.sem, 3)
                sp.wait_ge(qhi_done.sem, count_0)
                sp.wait_ge(taken(("p0", q)), count_1)
                sp.wait_ge(s0_full.sem, count_2)
                for hq in range(QH):
                    hi, lo = QHI[hq * DH:(hq + 1) * DH, q, :], QLO[hq * DH:(hq + 1) * DH, q, :]
                    h = q * QH + hq
                    stack(A0[:, h, :], B0[:, h, :], hi, lo, hi, lo, stack0_in[q][hq])

            def stack1(b):
                count_0 = held(sp, kqhi_done.at(b))
                count_1 = held(sp, other.nth_of_slot(("tq", 3), b + 1))
                count_2 = held(sp, s1_full.at(b - 1))
                sp.wait_ge(ident_set.sem, 3)
                sp.wait_ge(kqhi_done.sem, count_0)
                sp.wait_ge(taken(("tq", 3)), count_1)
                sp.wait_ge(s1_full.sem, count_2)
                for hq in range(QH):
                    own = slice(hq * DH, (hq + 1) * DH)
                    stack(A1[:, hq, :, :], B1[:, hq, :, :], KQHI[own, 1, :, :], KQLO[own, 1, :, :],
                          KQHI[own, 0, :, :], KQLO[own, 0, :, :], stack1_in[hq])

            def store(b):
                count_0 = held(sp, other.nth_of_slot(("w1", 1), b + 2))
                sp.wait_ge(ident_set.sem, 3)
                sp.wait_ge(taken(("w1", 1)), count_0)
                sp.dma_start(out_v[b], OUTT[:, :, :]).then_inc(stored.sem, 16)

            def iteration(i):
                if has(i, 1):
                    load_x(i + 1)
                if has(i, 0):
                    load_mask(i)
                if has(i, -2):
                    store(i - 2)
                if has(i, -1):
                    stack1(i - 1)
                if has(i, 1):
                    stack0(i + 1, 0)
                if has(i, 0):
                    load_residual(i)
                if has(i, 1):
                    stack0(i + 1, 1)

            def no_modulation():
                pass

            sp.dma_start(WQ[:, :, :], wq_t.rearrange("(c p) n -> p c n", p=P)).then_inc(wq_in.sem, 16)
            pipeline(sp, iteration, no_modulation)
            sp.wait_ge(stored.sem, 16 * NB)


def kernel(x, cond_2048, L0_cond_Wq, L0_cond_Wo, L1_cond_W_emb, L1_cond_b_emb, L1_cond_g_norm, L1_cond_W_qkv,
           L1_cond_g_q, L1_cond_g_k, L1_cond_W_out):
    import concourse.bacc as _bacc
    from concourse.bass_utils import run_bass_kernel_spmd as _run

    def by_partition(v, n):
        return np.ascontiguousarray(np.asarray(v).reshape(n, P).T)

    c = np.asarray(cond_2048)
    arrays = {
        "x": np.ascontiguousarray(x),
        "cond": np.ascontiguousarray(c),
        "cond_t": np.ascontiguousarray(c.reshape(NB, 4, P).transpose(2, 1, 0)),
        "wq_t": np.ascontiguousarray(np.asarray(L0_cond_Wq).T),
        "wo_t": np.ascontiguousarray(np.asarray(L0_cond_Wo).T),
        "w_emb": np.ascontiguousarray(L1_cond_W_emb),
        "b_emb_t": by_partition(L1_cond_b_emb, 8),
        "g_norm_t": by_partition(L1_cond_g_norm, 4),
        "w_qkv": np.ascontiguousarray(L1_cond_W_qkv),
        "g_q_t": np.ascontiguousarray(np.tile(np.asarray(L1_cond_g_q), QH).reshape(P, 1)),
        "g_k_t": np.ascontiguousarray(np.tile(np.asarray(L1_cond_g_k), QH).reshape(P, 1)),
        "w_out": np.ascontiguousarray(L1_cond_W_out),
    }
    nc = _bacc.Bacc("TRN2", target_bir_lowering=False, num_devices=1)
    args = [nc.dram_tensor(n, a.shape, F32, kind="ExternalInput").ap() for n, a in arrays.items()]
    args.append(nc.dram_tensor("out", (NB, D0, T0), F32, kind="ExternalOutput").ap())
    cond_resid(nc, *args)
    r = _run(nc, [arrays], core_ids=[0])
    return r.results[0]["out"]
```

```python
from contextlib import ExitStack

import numpy as np

import concourse.bass as bass
from concourse import mybir

F32 = mybir.dt.float32
F32R = mybir.dt.float32r
ALU = mybir.AluOpType
ACT = mybir.ActivationFunctionType
AX = mybir.AxisListType

NB = 16
P = 128
D0, T0 = 256, 512
N1, DM = 256, 512
DH = 32
H0, H1 = D0 // DH, DM // DH
QH = 4
Q0, Q1 = H0 // QH, H1 // QH
KB0, KB1 = T0 // P, N1 // P
SCALE = float(DH) ** -0.5
SCALE_RAW = SCALE * DH
EPS = 1e-6
NEG = 1e30

MAX_IN = {"A": (6, 6, 4, 0), "B": (3, 4, 5, 4), "C": (4, 4, 4, 0)}
MAX_EARLY = QH * KB0 - sum(MAX_IN["C"])


LOOP = (3, NB - 2)


def units(seg, g, k):
    first, n = sum(MAX_IN[seg][:g]) + (MAX_EARLY if seg == "C" else 0), MAX_IN[seg][g]
    if seg == "B":
        return range(first + k * n // QH, first + (k + 1) * n // QH)
    return range(first + -(-k * n // QH), first + -(-(k + 1) * n // QH))


class Event:

    def __init__(self, sem, per):
        self.sem, self.per = sem, per

    def at(self, b, n=None):
        n = self.per if n is None else n
        if not isinstance(b, int):
            return b * self.per + n
        return max(0, min(b * self.per + n, NB * self.per))


class Turns:

    def __init__(self, n, uses):
        self.n, self.uses = n, uses
        self.place = {key: k for k, (key, _) in enumerate(uses)}

    def slot(self, key):
        return self.place[key] % self.n

    def _count(self, key, i, mine):
        def upto(i):
            n = 0
            for j in range(-1, i + 1):
                for k, (_, off) in enumerate(self.uses):
                    if (j < i or k <= self.place[key]) and 0 <= j + off < NB and mine(k):
                        n += 1
            return n
        if isinstance(i, int):
            return upto(i)
        per = upto(LOOP[0] + 1) - upto(LOOP[0])
        return i * per + (upto(LOOP[0]) - LOOP[0] * per)

    def nth(self, key, i):
        return self._count(key, i, lambda k: True)

    def nth_of_slot(self, key, i):
        return self._count(key, i, lambda k: k % self.n == self.slot(key))


def before(count, n):
    return max(0, count - n) if isinstance(count, int) else count - n


def cond_resid(nc, x, cond, cond_t, wq_t, wo_t, w_emb, b_emb_t, g_norm_t, w_qkv, g_q_t, g_k_t, w_out, out):
    x_v = x.rearrange("b (c p) t -> b p c t", p=P)
    out_v = out.rearrange("b (c p) t -> b p c t", p=P)
    ctx = ExitStack()
    with ctx:
        def sb(name, shape, dt=F32):
            return ctx.enter_context(nc.sbuf_tensor(name, shape, dt))

        def pb(name, shape):
            return ctx.enter_context(nc.psum_tensor(name, shape, F32))

        def ev(name, per):
            return Event(ctx.enter_context(nc.semaphore(name)), per)

        WQ = sb("WQ", [P, 2, D0])
        WO = sb("WO", [P, 2, D0])
        WQKV = sb("WQKV", [P, 4, 3 * DM])
        WOUT = sb("WOUT", [P, 4, DM])
        CT = sb("CT", [P, 4, NB])
        KBIAS = sb("KBIAS", [P, 4, NB])
        KCOL = sb("KCOL", [P, 4])
        BEMB = sb("BEMB", [P, 8])
        GN = sb("GN", [P, 4])
        GQK = sb("GQK", [P, 2])
        AMOD = sb("AMOD", [P, 4, NB])
        SMOD = sb("SMOD", [P, 4, NB])
        IDENT = sb("IDENT", [P, P])
        ONES = sb("ONES", [P, DH])
        A0 = sb("A0", [P, H0, T0], F32R)
        B0 = sb("B0", [P, H0, T0], F32R)
        XIN = sb("XIN", [P, 2, T0])
        CBM = sb("CBM", [P, T0])
        CBR = sb("CBR", [P, T0])
        XMC = sb("XMC", [P, 2, T0])
        XS = sb("XS", [P, 2])
        MEAN = sb("MEAN", [P, 2, NB])
        QHI = sb("QHI", [P, 2, T0], F32R)
        QLO = sb("QLO", [P, 2, T0], F32R)
        QF = sb("QF", [P, 2, T0])
        OUTT = sb("OUTT", [P, 2, DM])
        V0 = sb("V0", [P, 2, KB0, P])
        NM0 = sb("NM0", [P, 2, 16])
        NMT0 = sb("NMT0", [16, 2, P], F32R)
        A1 = sb("A1", [P, QH, Q1, N1], F32R)
        B1 = sb("B1", [P, QH, Q1, N1], F32R)
        X1 = sb("X1", [P, 2, DM])
        X1R = sb("X1R", [P, 2, DM])
        SS = sb("SS", [P, 2])
        RSTD = sb("RSTD", [P, 2])
        YSQ = sb("YSQ", [P, 2, DM])
        XNT = sb("XNT", [P, 4, N1])
        QK = sb("QK", [P, 2, 2 * DM])
        SSQ = sb("SSQ", [P, 2, 2 * H1])
        RQK = sb("RQK", [P, 2, 2 * H1])
        HALF = sb("HALF", [P, H1])
        KQHI = sb("KQHI", [P, 2, Q1, N1], F32R)
        KQLO = sb("KQLO", [P, 2, Q1, N1], F32R)
        V1 = sb("V1", [P, 2, DM])
        NM1 = sb("NM1", [P, 2 * H1])
        NMT1 = sb("NMT1", [2 * H1, P], F32R)
        R1 = sb("R1", [P, N1])
        OT = sb("OT", [P, Q1, N1])
        E = sb("E", [P, 2, QH, T0])
        WEMB = E[:, :, :, :].rearrange("p a h t -> p (a h t)").rearrange("p (c n) -> p c n", c=4)
        R0 = QK[:, 0, 0:T0]
        TT = QK[:, 0, T0:2 * T0]
        CINV = QK[:, 1, 0:T0]

        PM = [pb(f"PM{k}", [P, 512]) for k in range(2)]
        PS = [pb(f"PS{k}", [P, 512]) for k in range(2)]
        PO = pb("PO", [P, 512])
        PD = pb("PD", [P, 512])
        PX = [pb(f"PX{k}", [P, 512]) for k in range(2)]

        wq_in = ev("wq_in", 0)
        mod_in = ev("mod_in", 0)
        weights_in = ev("weights_in", 0)
        consts_set = ev("consts_set", 0)
        ident_set = ev("ident_set", 0)
        mod_full = ev("mod_full", 0)
        mod_done = ev("mod_done", 0)
        xin_in = ev("xin_in", 16)
        cbm_in = ev("cbm_in", 16)
        cbr_in = ev("cbr_in", 16)
        xres_in = ev("xres_in", 16)
        xm_done = ev("xm_done", 2)
        xs_done = ev("xs_done", 1)
        p0_full = ev("p0_full", 3)
        qhi_done = ev("qhi_done", 2)
        qlo_done = ev("qlo_done", 2)
        stack0_in = [[ev(f"stack0_in{q}{h}", 6 * 16) for h in range(QH)] for q in range(Q0)]
        t0_full = ev("t0_full", 2)
        m0_full = ev("m0_full", 32)
        n0_full = ev("n0_full", 2)
        row0_in = [ev(f"row0_in{q}", 16) for q in range(Q0)]
        s0_full = ev("s0_full", 32)
        kcol_done = ev("kcol_done", 1)
        cinv_done = ev("cinv_done", 1)
        recip0_done = ev("recip0_done", 4)
        rc_done = ev("rc_done", 2)
        tt_done = ev("tt_done", 2)
        m_done = ev("m_done", 2)
        ctx_done = ev("ctx_done", 2)
        w0_full = ev("w0_full", 2)
        ss_done = ev("ss_done", 2)
        ms_done = ev("ms_done", 1)
        rstd_done = ev("rstd_done", 1)
        y_done = [ev(f"y_done{t}", 1) for t in range(2)]
        x1r_done = ev("x1r_done", 1)
        t1_full = ev("t1_full", 2)
        p1_full = ev("p1_full", 4)
        v1_full = ev("v1_full", 2)
        ssq_done = ev("ssq_done", 4)
        msq_done = ev("msq_done", 4)
        rqk_done = ev("rqk_done", 4)
        qn_done = ev("qn_done", 4)
        tq_full = ev("tq_full", 4)
        kqhi_done = ev("kqhi_done", 4)
        stack1_in = [ev(f"stack1_in{h}", 6 * 16) for h in range(QH)]
        m1_full = ev("m1_full", 16)
        n1_full = ev("n1_full", 1)
        row1_in = ev("row1_in", 16)
        s1_full = ev("s1_full", 16)
        esum_done = ev("esum_done", 4)
        ot_done = ev("ot_done", 4)
        w1_full = ev("w1_full", 2)
        stored = ev("stored", 16)
        max_done = ctx.enter_context(nc.semaphore("max_done"))
        exp_done = ctx.enter_context(nc.semaphore("exp_done"))
        pv_done = ctx.enter_context(nc.semaphore("pv_done"))
        sum_done = ctx.enter_context(nc.semaphore("sum_done"))
        context_taken = ctx.enter_context(nc.semaphore("context_taken"))
        sums_taken = ctx.enter_context(nc.semaphore("sums_taken"))
        other_taken = [ctx.enter_context(nc.semaphore(f"other_taken{k}")) for k in range(2)]

        maxima = Turns(2, [(("A", u), 0) for u in range(16)] + [(("B", u), -1) for u in range(16)]
                       + [(("C", u), 1) for u in range(16)])
        scores = Turns(2, [(("A", u), 0) for u in range(16)] + [(("B", u), 0) for u in range(16)]
                       + [(("C", u), -1) for u in range(16)])
        probs = Turns(2, [(("A", g), 0) for g in range(4)] + [(("B", g), 0) for g in range(4)]
                      + [(("C", g), -1) for g in range(4)])
        context = Turns(1, [("A", 0), ("B", 0)] + [(("C", c), -1) for c in range(4)])
        other = Turns(2, [*[(("p1", k), -1) for k in range(4)], (("n0", 1), 0),
                          *[(("tq", k), -1) for k in range(4)], (("p0", 0), 1), (("p0", 1), 1), (("mean", 0), 1),
                          (("t0", 0), 1), (("w1", 0), -2), (("n1", 0), -1), (("v1", 0), -1), (("v1", 1), -1), (("t0", 1), 1), (("w1", 1), -2),
                          (("w0", 0), 0), (("w0", 1), 0), (("n0", 0), 1), (("t1", 0), 0), (("t1", 1), 0)])

        def key_sums(c):
            return KQLO[:, c % 2, :, :].bitcast(F32)

        def has(i, off):
            return not isinstance(i, int) or 0 <= i + off < NB

        def held(eng, count):
            return count if isinstance(count, int) else eng.to_reg(count)

        def taken(key):
            return other_taken[other.slot(key)]

        def pipeline(eng, iteration, after_first):
            iteration(-1)
            after_first()
            for i in range(LOOP[0]):
                iteration(i)
            with eng.Fori(*LOOP) as i:
                iteration(i)
            for i in range(LOOP[1], NB + 2):
                iteration(i)

        block = ctx.enter_context(nc.Block())

        @block.tensor
        def _(pe):
            mm, tp = nc.tensor.matmul, nc.tensor.transpose

            def modulation():
                pe.wait_ge(mod_in.sem, 16 * 4)
                for n in range(8):
                    for c in range(4):
                        last = mm(PS[0][:, n * NB:(n + 1) * NB], WEMB[:, c, n * P:(n + 1) * P], CT[:, c, :],
                                  start=(c == 0), stop=(c == 3))
                last.then_inc(mod_full.sem, 1)
                pe.wait_ge(mod_done.sem, 1)
                pe.wait_ge(weights_in.sem, 16 * 5)
                pe.wait_ge(consts_set.sem, 4)

            def project0(i, b, mt):
                if mt == 0:
                    pe.wait_ge(xm_done.sem, xm_done.at(b))
                pe.wait_ge(taken(("p0", mt)), before(other.nth_of_slot(("p0", mt), i), 1))
                bank = PX[other.slot(("p0", mt))]
                for c in range(2):
                    last = mm(bank[:, :], WQ[:, c, mt * P:(mt + 1) * P], XMC[:, c, :], start=(c == 0), stop=(c == 1))
                last.then_inc(p0_full.sem, 1)

            def project_mean(i, b):
                pe.wait_ge(taken(("mean", 0)), before(other.nth_of_slot(("mean", 0), i), 1))
                pe.wait_ge(xs_done.sem, xs_done.at(b))
                bank = PX[other.slot(("mean", 0))]
                for mt in range(2):
                    for c in range(2):
                        last = mm(bank[:, mt:mt + 1], WQ[:, c, mt * P:(mt + 1) * P], XS[:, c:c + 1],
                                  start=(c == 0), stop=(c == 1))
                last.then_inc(p0_full.sem, 1)

            def values0(i, b, mt):
                pe.wait_ge(taken(("t0", mt)), before(other.nth_of_slot(("t0", mt), i), 1))
                pe.wait_ge(taken(("p0", mt)), other.nth_of_slot(("p0", mt), b - 1))
                bank = PX[other.slot(("t0", mt))]
                for kb in range(KB0):
                    last = tp(bank[:, kb * P:(kb + 1) * P], QF[:, mt, kb * P:(kb + 1) * P], IDENT[:, :])
                last.then_inc(t0_full.sem, 1)

            def max0(seg, i, b, q, u):
                hq, kb = u // KB0, u % KB0
                h = q * QH + hq
                if kb == 0:
                    pe.wait_ge(stack0_in[q][hq].sem, stack0_in[q][hq].at(b))
                pe.wait_ge(max_done, before(maxima.nth((seg, u), i), 2))
                mm(PM[maxima.slot((seg, u))][:, :], A0[0:96, h, kb * P:(kb + 1) * P], B0[0:96, h, :],
                   start=True, stop=True).then_inc(m0_full.sem, 1)

            def max1(i, b, u):
                own, c = slice(u % QH * DH, (u % QH + 1) * DH), u // QH
                if u == 0:
                    pe.wait_ge(kqhi_done.sem, kqhi_done.at(b))
                pe.wait_ge(max_done, before(maxima.nth(("B", u), i), 2))
                bank = PM[maxima.slot(("B", u))]
                for qb in range(2):
                    last = mm(bank[:, qb * N1:(qb + 1) * N1], KQHI[own, 0, c, qb * P:(qb + 1) * P], KQHI[own, 1, c, :],
                              start=True, stop=True)
                last.then_inc(m1_full.sem, 1)

            def rows0(i, b, q):
                pe.wait_ge(taken(("n0", q)), before(other.nth_of_slot(("n0", q), i), 1))
                pe.wait_ge(max_done, maxima.nth(("AC"[q == 0], 15), i))
                tp(PX[other.slot(("n0", q))][0:16, 0:P], NM0[:, q, :], IDENT[:, :]).then_inc(n0_full.sem, 1)

            def rows1(i, b):
                pe.wait_ge(taken(("n1", 0)), before(other.nth_of_slot(("n1", 0), i), 1))
                pe.wait_ge(max_done, maxima.nth(("B", 15), i))
                tp(PX[other.slot(("n1", 0))][0:2 * H1, 0:P], NM1[:, :], IDENT[:, :]).then_inc(n1_full.sem, 1)

            def score0(seg, i, b, q, g, hq):
                u, h = g * QH + hq, q * QH + hq
                if g == 0:
                    pe.wait_ge(stack0_in[q][hq].sem, stack0_in[q][hq].at(b))
                if u == 0:
                    pe.wait_ge(row0_in[q].sem, row0_in[q].at(b))
                pe.wait_ge(exp_done, before(scores.nth((seg, u), i), 2))
                mm(PS[scores.slot((seg, u))][:, :], A0[0:97, h, g * P:(g + 1) * P], B0[0:97, h, :],
                   start=True, stop=True).then_inc(s0_full.sem, 1)

            def score1(i, b, c, hq):
                u = c * QH + hq
                if c == 0:
                    pe.wait_ge(stack1_in[hq].sem, stack1_in[hq].at(b))
                if u == 0:
                    pe.wait_ge(row1_in.sem, row1_in.at(b))
                pe.wait_ge(exp_done, before(scores.nth(("C", u), i), 2))
                bank = PS[scores.slot(("C", u))]
                for kb in range(KB1):
                    last = mm(bank[:, kb * N1:(kb + 1) * N1], A1[0:97, hq, c, kb * P:(kb + 1) * P], B1[0:97, hq, c, :],
                              start=True, stop=True)
                last.then_inc(s1_full.sem, 1)

            def values_weighted0(seg, i, q, g):
                if g == 0:
                    pe.wait_ge(context_taken, before(context.nth(seg, i), 1))
                    pe.wait_ge(taken(("t0", q)), other.nth_of_slot(("t0", q), i - 1))
                pe.wait_ge(exp_done, scores.nth((seg, QH * g + QH - 1), i))
                for h in range(QH):
                    last = mm(PO[h * DH:(h + 1) * DH, :], V0[:, q, g, h * DH:(h + 1) * DH],
                              E[:, probs.slot((seg, g)), h, :], start=(g == 0), stop=(g == KB0 - 1))
                last.then_inc(pv_done, 1)

            def weights_summed0(seg, i, g):
                if g == 0:
                    pe.wait_ge(sums_taken, before(context.nth(seg, i), 1))
                for h in range(QH):
                    last = mm(PD[h * DH:(h + 1) * DH, :], ONES[:, :], E[:, probs.slot((seg, g)), h, :],
                              start=(g == 0), stop=(g == KB0 - 1))
                last.then_inc(sum_done, 1)

            def values_weighted1(i, c):
                pe.wait_ge(context_taken, before(context.nth(("C", c), i), 1))
                if c == 0:
                    pe.wait_ge(taken(("v1", 0)), other.nth_of_slot(("v1", 0), i))
                    pe.wait_ge(taken(("v1", 1)), other.nth_of_slot(("v1", 1), i))
                pe.wait_ge(exp_done, scores.nth(("C", QH * c + QH - 1), i))
                for kb in range(KB1):
                    for h in range(QH):
                        last = mm(PO[h * DH:(h + 1) * DH, 0:N1], V1[:, kb, c * P + h * DH:c * P + (h + 1) * DH],
                                  E[:, probs.slot(("C", c)), h, kb * N1:(kb + 1) * N1],
                                  start=(kb == 0), stop=(kb == KB1 - 1))
                last.then_inc(pv_done, 1)

            def weights_summed1(i, b, c):
                pe.wait_ge(sums_taken, before(context.nth(("C", c), i), 1))
                pe.wait_ge(esum_done.sem, esum_done.at(b, c + 1))
                for h in range(QH):
                    last = mm(PD[h * DH:(h + 1) * DH, 0:N1], ONES[:, :], key_sums(c)[:, h, :], start=True, stop=True)
                last.then_inc(sum_done, 1)

            def out0(i, b, mt):
                pe.wait_ge(ctx_done.sem, ctx_done.at(b))
                pe.wait_ge(taken(("w0", mt)), before(other.nth_of_slot(("w0", mt), i), 1))
                bank = PX[other.slot(("w0", mt))]
                for c in range(2):
                    last = mm(bank[:, :], WO[:, c, mt * P:(mt + 1) * P], XMC[:, c, :], start=(c == 0), stop=(c == 1))
                last.then_inc(w0_full.sem, 1)

            def norm_rows(i, b):
                pe.wait_ge(y_done[0].sem, y_done[0].at(b))
                pe.wait_ge(y_done[1].sem, y_done[1].at(b))
                for k in range(2):
                    pe.wait_ge(taken(("t1", k)), before(other.nth_of_slot(("t1", k), i), 1))
                    bank = PX[other.slot(("t1", k))]
                    for cc in range(2):
                        for t in range(2):
                            c = 2 * k + cc
                            last = tp(bank[:, (2 * cc + t) * P:(2 * cc + t + 1) * P], YSQ[:, t, c * P:(c + 1) * P],
                                      IDENT[:, :])
                    last.then_inc(t1_full.sem, 1)

            def project1(i, b, key, t, part, event):
                pe.wait_ge(taken(key), before(other.nth_of_slot(key, i), 1))
                if key == ("p1", 0):
                    pe.wait_ge(taken(("t1", 1)), other.nth_of_slot(("t1", 1), i - 1))
                bank = PX[other.slot(key)]
                for c in range(4):
                    last = mm(bank[:, :], XNT[:, c, t * P:(t + 1) * P], WQKV[:, c, part * DM:(part + 1) * DM],
                              start=(c == 0), stop=(c == 3))
                last.then_inc(event.sem, 1)

            def heads_rows(i, b, part):
                pe.wait_ge(qn_done.sem, qn_done.at(b))
                for k in range(2):
                    key = ("tq", 2 * part + k)
                    pe.wait_ge(taken(key), before(other.nth_of_slot(key, i), 1))
                    bank = PX[other.slot(key)]
                    for cc in range(2):
                        for t in range(2):
                            c = 2 * k + cc
                            last = tp(bank[:, (2 * cc + t) * P:(2 * cc + t + 1) * P],
                                      QK[:, t, part * DM + c * P:part * DM + (c + 1) * P], IDENT[:, :])
                    last.then_inc(tq_full.sem, 1)

            def out1(i, b, t):
                pe.wait_ge(ot_done.sem, ot_done.at(b))
                pe.wait_ge(taken(("w1", t)), before(other.nth_of_slot(("w1", t), i), 1))
                bank = PX[other.slot(("w1", t))]
                for c in range(4):
                    last = mm(bank[:, :], OT[:, c, t * P:(t + 1) * P], WOUT[:, c, :], start=(c == 0), stop=(c == 3))
                last.then_inc(w1_full.sem, 1)

            def iteration(i):
                def step_a(g, k):
                    if has(i, 0):
                        score0("A", i, i, 0, g, k)
                        for u in units("A", g, k):
                            max0("A", i, i, 1, u)

                def step_b(g, k):
                    if has(i, 0):
                        score0("B", i, i, 1, g, k)
                    if has(i, -1):
                        for u in units("B", g, k):
                            max1(i, i - 1, u)

                def step_c(g, k):
                    if has(i, -1):
                        score1(i, i - 1, g, k)
                    if has(i, 1):
                        for u in units("C", g, k):
                            max0("C", i, i + 1, 0, u)

                step_a(0, 0)
                if has(i, -2):
                    values_weighted1(i - 1, 3)
                step_a(0, 1)
                if has(i, -1):
                    project1(i, i - 1, ("p1", 0), 0, 0, p1_full)
                step_a(0, 2)
                if has(i, -2):
                    weights_summed1(i - 1, i - 2, 3)
                step_a(0, 3)
                if has(i, -1):
                    project1(i, i - 1, ("p1", 1), 0, 1, p1_full)
                step_a(1, 0)
                if has(i, 0):
                    values_weighted0("A", i, 0, 0)
                step_a(1, 1)
                if has(i, -1):
                    project1(i, i - 1, ("p1", 2), 1, 0, p1_full)
                step_a(1, 2)
                if has(i, 0):
                    weights_summed0("A", i, 0)
                step_a(1, 3)
                if has(i, -1):
                    project1(i, i - 1, ("p1", 3), 1, 1, p1_full)
                step_a(2, 0)
                if has(i, 0):
                    values_weighted0("A", i, 0, 1)
                step_a(2, 1)
                step_a(2, 2)
                if has(i, 0):
                    weights_summed0("A", i, 1)
                step_a(2, 3)
                step_a(3, 0)
                step_a(3, 1)
                if has(i, 0):
                    rows0(i, i, 1)
                    values_weighted0("A", i, 0, 2)
                if has(i, -1):
                    heads_rows(i, i - 1, 0)
                step_a(3, 2)
                if has(i, 0):
                    weights_summed0("A", i, 2)
                step_a(3, 3)
                if has(i, -1):
                    heads_rows(i, i - 1, 1)

                step_b(0, 0)
                if has(i, 0):
                    values_weighted0("A", i, 0, 3)
                step_b(0, 1)
                if has(i, 1):
                    project0(i, i + 1, 0)
                step_b(0, 2)
                if has(i, 1):
                    project0(i, i + 1, 1)
                    project_mean(i, i + 1)
                step_b(0, 3)
                if has(i, 0):
                    weights_summed0("A", i, 3)
                step_b(1, 0)
                if has(i, 1):
                    values0(i, i + 1, 0)
                for g in range(1, 4):
                    if g > 1:
                        step_b(g, 0)
                    step_b(g, 1)
                    if has(i, 0):
                        values_weighted0("B", i, 1, g - 1)
                    step_b(g, 2)
                    if g == 2 and has(i, -2):
                        out1(i, i - 2, 0)
                    step_b(g, 3)
                    if has(i, 0):
                        weights_summed0("B", i, g - 1)
                if has(i, -1):
                    rows1(i, i - 1)
                if has(i, 1):
                    for u in range(MAX_EARLY // 2):
                        max0("C", i, i + 1, 0, u)
                if has(i, -1):
                    project1(i, i - 1, ("v1", 0), 0, 2, v1_full)
                if has(i, 1):
                    for u in range(MAX_EARLY // 2, MAX_EARLY):
                        max0("C", i, i + 1, 0, u)

                step_c(0, 0)
                step_c(0, 1)
                if has(i, 0):
                    values_weighted0("B", i, 1, 3)
                step_c(0, 2)
                if has(i, -1):
                    project1(i, i - 1, ("v1", 1), 1, 2, v1_full)
                step_c(0, 3)
                if has(i, 0):
                    weights_summed0("B", i, 3)
                step_c(1, 0)
                if has(i, 1):
                    values0(i, i + 1, 1)
                if has(i, -2):
                    out1(i, i - 2, 1)
                for g in range(1, 4):
                    if g > 1:
                        step_c(g, 0)
                    if g == 3 and has(i, 1):
                        rows0(i, i + 1, 0)
                    step_c(g, 1)
                    if has(i, -1):
                        values_weighted1(i, g - 1)
                    step_c(g, 2)
                    step_c(g, 3)
                    if has(i, -1):
                        weights_summed1(i, i - 1, g - 1)
                    if g == 2 and has(i, 0):
                        out0(i, i, 0)
                        out0(i, i, 1)
                if has(i, 0):
                    norm_rows(i, i)

            pe.wait_ge(wq_in.sem, 16)
            pe.wait_ge(ident_set.sem, 3)
            pipeline(pe, iteration, modulation)

        @block.scalar
        def _(act):
            fn = nc.scalar.activation

            def copy(o, i_):
                return fn(o, i_, ACT.Copy)

            def key_bias(i, b):
                count_0 = held(act, scores.nth(("B", 15), i - 1))
                act.wait_ge(ident_set.sem, 3)
                act.wait_ge(exp_done, count_0)
                copy(KCOL[:, :].unsqueeze(2), KBIAS[:, :, bass.ds(b, 1)]).then_inc(kcol_done.sem, 1)
                act.wait_ge(kcol_done.sem, kcol_done.at(b))

            def exp0(seg, i, b, q, g, h):
                if h == 0:
                    act.wait_ge(sum_done, before(probs.nth((seg, g), i), 2))
                u = g * QH + h
                act.wait_ge(s0_full.sem, s0_full.at(b, 16 * q + u + 1))
                fn(E[:, probs.slot((seg, g)), h, :], PS[scores.slot((seg, u))][:, :], ACT.Exp,
                   bias=KCOL[:, g:g + 1], scale=SCALE).then_inc(exp_done, 1)

            def exp1(i, b, c, h):
                if h == 0:
                    act.wait_ge(sum_done, before(probs.nth(("C", c), i), 2))
                u = c * QH + h
                act.wait_ge(s1_full.sem, s1_full.at(b, u + 1))
                fn(E[:, probs.slot(("C", c)), h, :], PS[scores.slot(("C", u))][:, :], ACT.Exp,
                   scale=SCALE_RAW).then_inc(exp_done, 1)

            def take_context0(seg, i, b, q):
                act.wait_ge(pv_done, probs.nth((seg, 3), i))
                act.wait_ge(tq_full.sem, tq_full.at(b - 1))
                act.wait_ge(ctx_done.sem, ctx_done.at(b, q))
                copy(TT, PO[:, :]).then_inc(context_taken, 1)

            def take_context1(i, b, c):
                act.wait_ge(pv_done, probs.nth(("C", c), i))
                if c == 0:
                    act.wait_ge(w1_full.sem, w1_full.at(b - 1))
                copy(OT[:, c, :], PO[:, 0:N1]).then_inc(context_taken, 1)

            def split0(i, b, mt):
                bank = PX[other.slot(("p0", mt))]
                act.wait_ge(p0_full.sem, p0_full.at(b, mt + 1))
                for h in range(QH):
                    act.wait_ge(stack0_in[mt][h].sem, stack0_in[mt][h].at(b - 1))
                copy(QHI[:, mt, :], bank[:, :]).then_inc(qhi_done.sem, 1)
                act.wait_ge(t0_full.sem, t0_full.at(b - 1, mt + 1))
                act.wait_ge(qlo_done.sem, qlo_done.at(b - 1, mt + 1))
                copy(QF[:, mt, :], bank[:, :]).then_inc(taken(("p0", mt)), 1)

            def mean0(i, b):
                count_0 = held(act, p0_full.at(b, 3))
                act.wait_ge(ident_set.sem, 3)
                act.wait_ge(p0_full.sem, count_0)
                fn(MEAN[:, :, bass.ds(b, 1)], PX[other.slot(("mean", 0))][:, 0:2].rearrange("p (a o) -> p a o", o=1),
                   ACT.Copy, scale=1.0 / T0).then_inc(taken(("mean", 0)), 1)

            def values0(i, b, mt):
                act.wait_ge(t0_full.sem, t0_full.at(b, mt + 1))
                act.wait_ge(pv_done, probs.nth(("AB"[mt], 3), i))
                copy(V0[:, mt, :, :], PX[other.slot(("t0", mt))][:, :].rearrange("p (k d) -> p k d", k=KB0)) \
                    .then_inc(taken(("t0", mt)), 1)

            def rows0(i, b, q):
                act.wait_ge(n0_full.sem, n0_full.at(b, 1 if q == 0 else 2))
                act.wait_ge(row0_in[q].sem, row0_in[q].at(b - 1))
                copy(NMT0[:, q, :], PX[other.slot(("n0", q))][0:16, 0:P]).then_inc(taken(("n0", q)), 1)
                act.wait_ge(taken(("n0", q)), other.nth_of_slot(("n0", q), i))
                act.dma_start(B0[96:97, q * QH:(q + 1) * QH, :].rearrange("p h (k t) -> p (h k) t", t=P).bitcast(F32),
                              NMT0[:, q, :].bitcast(F32)).then_inc(row0_in[q].sem, 16)

            def rows1(i, b):
                act.wait_ge(n1_full.sem, n1_full.at(b))
                act.wait_ge(row1_in.sem, row1_in.at(b - 1))
                copy(NMT1[:, :], PX[other.slot(("n1", 0))][0:2 * H1, 0:P]).then_inc(taken(("n1", 0)), 1)
                act.wait_ge(taken(("n1", 0)), other.nth_of_slot(("n1", 0), i))
                act.dma_start(B1[96:97, :, :, :].rearrange("p h c (k t) -> p (h c k) t", t=P).bitcast(F32),
                              NMT1[:, :].bitcast(F32)).then_inc(row1_in.sem, 16)

            def heads(i, b, k):
                bank = PX[other.slot(("p1", k))]
                act.wait_ge(p1_full.sem, p1_full.at(b, k + 1))
                if k == 0:
                    act.wait_ge(ctx_done.sem, ctx_done.at(b))
                    act.wait_ge(tq_full.sem, tq_full.at(b - 1))
                    act.wait_ge(t1_full.sem, t1_full.at(b))
                copy(QK[:, k // 2, (k % 2) * DM:(k % 2 + 1) * DM], bank[:, :])
                if k >= 2:
                    act.wait_ge(ssq_done.sem, ssq_done.at(b, k - 1))
                fn(YSQ[:, k % 2, :], bank[:, :], ACT.Square).then_inc(taken(("p1", k)), 1)

            def values1(i, b, t):
                act.wait_ge(v1_full.sem, v1_full.at(b, t + 1))
                act.wait_ge(pv_done, probs.nth(("C", 3), i - 1))
                copy(V1[:, t, :], PX[other.slot(("v1", t))][:, :]).then_inc(taken(("v1", t)), 1)

            def split1(i, b, part):
                for k in (2 * part, 2 * part + 1):
                    act.wait_ge(tq_full.sem, tq_full.at(b, k + 1))
                    if k == 0:
                        act.wait_ge(m1_full.sem, m1_full.at(b - 1))
                        for h in range(QH):
                            act.wait_ge(stack1_in[h].sem, stack1_in[h].at(b - 1))
                    fn(KQHI[:, part, 2 * (k % 2):2 * (k % 2) + 2, :],
                       PX[other.slot(("tq", k))][:, :].rearrange("p (c t) -> p c t", c=2),
                       ACT.Copy, scale=GQK[:, part:part + 1]).then_inc(kqhi_done.sem, 1)

            def keep_x1(i, b):
                act.wait_ge(taken(("w1", 1)), other.nth_of_slot(("w1", 1), i))
                act.wait_ge(taken(("w1", 0)), other.nth_of_slot(("w1", 0), i))
                copy(X1R[:, :, :], X1[:, :, :]).then_inc(x1r_done.sem, 1)

            def squares(i, b, t):
                if t == 0:
                    act.wait_ge(ssq_done.sem, ssq_done.at(b - 1))
                    act.wait_ge(t1_full.sem, t1_full.at(b - 1))
                    act.wait_ge(rstd_done.sem, rstd_done.at(b - 1))
                act.wait_ge(taken(("w0", t)), other.nth_of_slot(("w0", t), i))
                fn(YSQ[:, t, :], X1[:, t, :], ACT.Square, accum_out=SS[:, t:t + 1]).then_inc(ss_done.sem, 1)

            def norm(i, b):
                act.wait_ge(rstd_done.sem, rstd_done.at(b))
                fn(YSQ[:, 0, :], X1[:, 0, :], ACT.Copy, scale=RSTD[:, 0:1]).then_inc(y_done[0].sem, 1)

            def iteration(i):
                def step_a(g, *heads_):
                    if has(i, 0):
                        for h in heads_:
                            exp0("A", i, i, 0, g, h)

                def step_b(g, *heads_):
                    if has(i, 0):
                        for h in heads_:
                            exp0("B", i, i, 1, g, h)

                def step_c(g, *heads_):
                    if has(i, -1):
                        for h in heads_:
                            exp1(i, i - 1, g, h)

                if has(i, 0):
                    key_bias(i, i)
                step_a(0, 0)
                if has(i, -2):
                    take_context1(i - 1, i - 2, 3)
                step_a(0, 1)
                if has(i, -1):
                    heads(i, i - 1, 0)
                step_a(0, 2, 3)
                if has(i, -1):
                    heads(i, i - 1, 1)
                step_a(1, 0, 1)
                if has(i, -1):
                    heads(i, i - 1, 2)
                step_a(1, 2, 3)
                if has(i, -1):
                    heads(i, i - 1, 3)
                step_a(2, 0, 1, 2, 3)
                step_a(3, 0, 1)
                if has(i, 0):
                    rows0(i, i, 1)
                if has(i, -1):
                    split1(i, i - 1, 0)
                step_a(3, 2, 3)
                if has(i, -1):
                    split1(i, i - 1, 1)
                step_b(0, 0)
                if has(i, 0):
                    take_context0("A", i, i, 0)
                step_b(0, 1)
                if has(i, 1):
                    split0(i, i + 1, 0)
                step_b(0, 2)
                if has(i, 1):
                    split0(i, i + 1, 1)
                    mean0(i, i + 1)
                step_b(0, 3)
                step_b(1, 0)
                if has(i, 1):
                    values0(i, i + 1, 0)
                step_b(1, 1, 2, 3)
                step_b(2, 0, 1, 2, 3)
                step_b(3, 0, 1, 2, 3)
                if has(i, -1):
                    rows1(i, i - 1)
                    values1(i, i - 1, 0)
                step_c(0, 0, 1)
                if has(i, 0):
                    take_context0("B", i, i, 1)
                step_c(0, 2)
                if has(i, -1):
                    values1(i, i - 1, 1)
                step_c(0, 3)
                step_c(1, 0)
                if has(i, 1):
                    values0(i, i + 1, 1)
                step_c(1, 1)
                if has(i, -1):
                    take_context1(i, i - 1, 0)
                step_c(1, 2, 3)
                if has(i, -1):
                    keep_x1(i, i - 1)
                step_c(2, 0, 1)
                if has(i, -1):
                    take_context1(i, i - 1, 1)
                step_c(2, 2, 3)
                if has(i, 0):
                    squares(i, i, 0)
                step_c(3, 0)
                if has(i, 0):
                    squares(i, i, 1)
                step_c(3, 1)
                if has(i, 1):
                    rows0(i, i + 1, 0)
                if has(i, 0):
                    norm(i, i)
                if has(i, -1):
                    take_context1(i, i - 1, 2)
                step_c(3, 2, 3)

            def loads():
                act.wait_ge(wq_in.sem, 16)
                act.wait_ge(xin_in.sem, xin_in.at(0))
                for dst, src in ((CT[:, :, :], cond_t), (WEMB, w_emb.rearrange("(c p) n -> p c n", p=P)),
                                 (BEMB[:, :], b_emb_t), (GN[:, :], g_norm_t)):
                    act.dma_start(dst, src).then_inc(mod_in.sem, 16)
                for dst, src in ((WO[:, :, :], wo_t.rearrange("(c p) n -> p c n", p=P)),
                                 (WQKV[:, :, :], w_qkv.rearrange("(c p) n -> p c n", p=P)),
                                 (WOUT[:, :, :], w_out.rearrange("(c p) n -> p c n", p=P)),
                                 (GQK[:, 0:1], g_q_t), (GQK[:, 1:2], g_k_t)):
                    act.dma_start(dst, src).then_inc(weights_in.sem, 16)

            def modulation():
                act.wait_ge(weights_in.sem, 16 * 5)
                act.wait_ge(consts_set.sem, 4)
                act.wait_ge(mod_done.sem, 1)

            loads()
            pipeline(act, iteration, modulation)

        @block.vector
        def _(dve):
            v = nc.vector

            def constants():
                v.memset(ONES[:, :], 1.0).then_inc(consts_set.sem, 1)
                v.memset(A0[96:97, :, :].bitcast(F32), 1.0).then_inc(consts_set.sem, 1)
                v.memset(A1[96:97, :, :, :].bitcast(F32), 1.0).then_inc(consts_set.sem, 1)
                dve.wait_ge(ident_set.sem, 3)

            def modulation():
                dve.wait_ge(mod_in.sem, 16 * 4)
                dve.wait_ge(weights_in.sem, 16 * 5)
                v.tensor_scalar(KBIAS[:, :, :], CT[:, :, :], 1.0, NEG, ALU.subtract, ALU.mult).then_inc(consts_set.sem, 1)
                for c in range(4):
                    blk = WOUT[:, c, c * P:(c + 1) * P]
                    v.tensor_tensor(blk, blk, IDENT[:, :], ALU.add)
                dve.wait_ge(mod_full.sem, 1)
                for n in range(4):
                    v.tensor_scalar(AMOD[:, n, :], PS[0][:, n * NB:(n + 1) * NB], BEMB[:, n:n + 1], 1.0, ALU.add, ALU.add)
                for n in range(4):
                    last = v.tensor_scalar(SMOD[:, n, :], PS[0][:, (4 + n) * NB:(5 + n) * NB], BEMB[:, 4 + n:5 + n], None,
                                           ALU.add)
                last.then_inc(mod_done.sem, 1)
                dve.wait_ge(mod_done.sem, 1)
                for n in range(4):
                    last = v.tensor_scalar(AMOD[:, n, :], AMOD[:, n, :], GN[:, n:n + 1], float(DM) ** 0.5,
                                           ALU.mult, ALU.mult)
                last.then_inc(mod_done.sem, 1)
                dve.wait_ge(mod_done.sem, 2)

            def sums_x(i, b):
                dve.wait_ge(xin_in.sem, xin_in.at(b))
                dve.wait_ge(p0_full.sem, p0_full.at(b - 1))
                v.reduce_sum(XS[:, :], XIN[:, :, :], AX.X).then_inc(xs_done.sem, 1)

            def max0(seg, i, b, q, u):
                if u == 0:
                    dve.wait_ge(n0_full.sem, n0_full.at(b - 1, q + 1))
                dve.wait_ge(m0_full.sem, m0_full.at(b, 16 * q + u + 1))
                v.tensor_reduce(NM0[:, q, u:u + 1], PM[maxima.slot((seg, u))][:, :], axis=AX.X, op=ALU.max,
                                negate=True).then_inc(max_done, 1)

            def max1(i, b, u):
                k = u % QH * Q1 + u // QH
                if u == 0:
                    dve.wait_ge(n1_full.sem, n1_full.at(b - 1))
                dve.wait_ge(m1_full.sem, m1_full.at(b, u + 1))
                v.tensor_reduce(NM1[:, 2 * k:2 * k + 2],
                                PM[maxima.slot(("B", u))][:, :].rearrange("p (a k) -> p a k", a=2), axis=AX.X,
                                op=ALU.max, negate=True).then_inc(max_done, 1)

            def split0(i, b, mt):
                dve.wait_ge(taken(("p0", mt)), other.nth_of_slot(("p0", mt), i))
                for h in range(QH):
                    dve.wait_ge(stack0_in[mt][h].sem, stack0_in[mt][h].at(b - 1))
                v.tensor_tensor(QLO[:, mt, :], QF[:, mt, :], QHI[:, mt, :].bitcast(F32),
                                ALU.subtract).then_inc(qlo_done.sem, 1)

            def take_sums0(i, b, q):
                dve.wait_ge(sum_done, probs.nth(("AB"[q], 3), i))
                dve.wait_ge(cinv_done.sem, cinv_done.at(b))
                dve.wait_ge(ctx_done.sem, ctx_done.at(b, q))
                dve.wait_ge(tq_full.sem, tq_full.at(b - 1))
                v.tensor_tensor(R0, PD[:, :], CINV, ALU.add).then_inc(sums_taken, 1)
                dve.wait_ge(p0_full.sem, p0_full.at(b + 1))
                dve.wait_ge(taken(("mean", 0)), other.nth_of_slot(("mean", 0), i - 1))
                dve.wait_ge(w0_full.sem, w0_full.at(b - 1))
                v.tensor_scalar(XMC[:, q, :], CINV, MEAN[:, q, bass.ds(b, 1)], None, ALU.mult).then_inc(m_done.sem, 1)

            def invert0(i, b, q, half):
                dve.wait_ge(sums_taken, context.nth("AB"[q], i))
                r0 = R0[:, half * (T0 // 2):(half + 1) * (T0 // 2)]
                v.reciprocal(r0, r0).then_inc(recip0_done.sem, 1)

            def residual0(i, b):
                dve.wait_ge(xres_in.sem, xres_in.at(b))
                for mt in range(2):
                    dve.wait_ge(w0_full.sem, w0_full.at(b, mt + 1))
                    v.tensor_tensor(X1[:, mt, :], PX[other.slot(("w0", mt))][:, :], X1[:, mt, :], ALU.add) \
                        .then_inc(taken(("w0", mt)), 1)

            def mean_square(i, b):
                dve.wait_ge(ss_done.sem, ss_done.at(b))
                dve.wait_ge(y_done[0].sem, y_done[0].at(b - 1))
                dve.wait_ge(y_done[1].sem, y_done[1].at(b - 1))
                v.tensor_scalar(RSTD[:, :], SS[:, :], DM * EPS, None, ALU.add).then_inc(ms_done.sem, 1)

            def norm(i, b):
                dve.wait_ge(rstd_done.sem, rstd_done.at(b))
                v.tensor_scalar(YSQ[:, 1, :], X1[:, 1, :], RSTD[:, 1:2], None, ALU.mult).then_inc(y_done[1].sem, 1)

            def modulate(i, b):
                dve.wait_ge(v1_full.sem, v1_full.at(b - 1))
                for k in range(2):
                    dve.wait_ge(t1_full.sem, t1_full.at(b, k + 1))
                    for cc in range(2):
                        c = 2 * k + cc
                        last = v.tensor_scalar(XNT[:, c, :], PX[other.slot(("t1", k))][:, cc * N1:(cc + 1) * N1],
                                               AMOD[:, c, bass.ds(b, 1)], SMOD[:, c, bass.ds(b, 1)],
                                               ALU.mult, ALU.add)
                    last.then_inc(taken(("t1", k)), 1)

            def square_sums(i, b, k):
                own = slice(k % 2 * H1, (k % 2 + 1) * H1)
                dve.wait_ge(taken(("p1", k)), other.nth_of_slot(("p1", k), i))
                dve.wait_ge(msq_done.sem, msq_done.at(b - 1, k + 1))
                v.reduce_sum(SSQ[:, k // 2, own], YSQ[:, k % 2, :].rearrange("p (h d) -> p h d", d=DH), AX.X) \
                    .then_inc(ssq_done.sem, 1)
                dve.wait_ge(ssq_done.sem, ssq_done.at(b, k + 1))
                dve.wait_ge(qn_done.sem, qn_done.at(b - 1, k + 1))
                v.tensor_scalar(RQK[:, k // 2, own], SSQ[:, k // 2, own], DH * EPS, None, ALU.add) \
                    .then_inc(msq_done.sem, 1)

            def split1(i, b, part):
                for k in (2 * part, 2 * part + 1):
                    dve.wait_ge(kqhi_done.sem, kqhi_done.at(b, k + 1))
                    own = slice(2 * (k % 2), 2 * (k % 2) + 2)
                    v.scalar_tensor_tensor(out=KQLO[:, part, own, :].rearrange("p c t -> p (c t)"),
                                           in0=PX[other.slot(("tq", k))][:, :], scalar=GQK[:, part:part + 1],
                                           in1=KQHI[:, part, own, :].rearrange("p c t -> p (c t)").bitcast(F32),
                                           op0=ALU.mult, op1=ALU.subtract).then_inc(taken(("tq", k)), 1)

            def context1(i, b, c):
                dve.wait_ge(sum_done, probs.nth(("C", c), i))
                dve.wait_ge(ot_done.sem, ot_done.at(b, c))
                v.reciprocal(R1[:, :], PD[:, 0:N1]).then_inc(sums_taken, 1)
                dve.wait_ge(sums_taken, context.nth(("C", c), i))
                dve.wait_ge(context_taken, context.nth(("C", c), i))
                v.tensor_tensor(OT[:, c, :], OT[:, c, :], R1[:, :], ALU.mult).then_inc(ot_done.sem, 1)

            def residual1(i, b, t):
                if t == 0:
                    dve.wait_ge(x1r_done.sem, x1r_done.at(b))
                    dve.wait_ge(stored.sem, stored.at(b - 1))
                dve.wait_ge(w1_full.sem, w1_full.at(b, t + 1))
                v.tensor_tensor(OUTT[:, t, :], PX[other.slot(("w1", t))][:, :], X1R[:, t, :], ALU.add) \
                    .then_inc(taken(("w1", t)), 1)

            def iteration(i):
                def step_a(g, *steps):
                    if has(i, 0):
                        for k in steps:
                            for u in units("A", g, k):
                                max0("A", i, i, 1, u)

                def step_b(g, *steps):
                    if has(i, -1):
                        for k in steps:
                            for u in units("B", g, k):
                                max1(i, i - 1, u)

                def step_c(g, *steps):
                    if has(i, 1):
                        for k in steps:
                            for u in units("C", g, k):
                                max0("C", i, i + 1, 0, u)

                step_a(0, 0)
                if has(i, -2):
                    context1(i - 1, i - 2, 2)
                step_a(0, 1, 2)
                if has(i, -1):
                    square_sums(i, i - 1, 0)
                if has(i, -2):
                    context1(i - 1, i - 2, 3)
                step_a(0, 3)
                if has(i, 1):
                    sums_x(i, i + 1)
                step_a(1, 0)
                if has(i, -1):
                    square_sums(i, i - 1, 1)
                step_a(1, 1, 2)
                if has(i, -1):
                    square_sums(i, i - 1, 2)
                step_a(1, 3)
                step_a(2, 0)
                if has(i, -1):
                    square_sums(i, i - 1, 3)
                step_a(2, 1, 2, 3)
                if has(i, -1):
                    split1(i, i - 1, 0)
                    split1(i, i - 1, 1)
                step_b(0, 0, 1)
                if has(i, 1):
                    split0(i, i + 1, 0)
                step_b(0, 2)
                if has(i, 1):
                    split0(i, i + 1, 1)
                step_b(0, 3)
                if has(i, 0):
                    take_sums0(i, i, 0)
                step_b(1, 0, 1, 2, 3)
                step_b(2, 0, 1, 2)
                if has(i, 0):
                    invert0(i, i, 0, 0)
                if has(i, -2):
                    residual1(i, i - 2, 0)
                step_b(2, 3)
                step_b(3, 0, 1, 2, 3)
                if has(i, 1):
                    for u in range(MAX_EARLY // 2):
                        max0("C", i, i + 1, 0, u)
                if has(i, 0):
                    invert0(i, i, 0, 1)
                if has(i, 1):
                    for u in range(MAX_EARLY // 2, MAX_EARLY):
                        max0("C", i, i + 1, 0, u)
                step_c(0, 0, 1, 2, 3)
                if has(i, 0):
                    take_sums0(i, i, 1)
                step_c(1, 0)
                if has(i, 0):
                    invert0(i, i, 1, 0)
                    invert0(i, i, 1, 1)
                if has(i, -2):
                    residual1(i, i - 2, 1)
                step_c(1, 1, 2, 3)
                step_c(2, 0, 1)
                if has(i, -1):
                    context1(i, i - 1, 0)
                step_c(2, 2, 3)
                if has(i, -1):
                    context1(i, i - 1, 1)
                if has(i, 0):
                    residual0(i, i)
                    mean_square(i, i)
                    norm(i, i)
                    modulate(i, i)

            constants()
            pipeline(dve, iteration, modulation)

        @block.gpsimd
        def _(pool):
            g = nc.gpsimd

            def identity():
                g.memset(HALF[:, :], -0.5).then_inc(ident_set.sem, 1)
                g.memset(IDENT[:, :], 0.0).then_inc(ident_set.sem, 1)
                pool.wait_ge(ident_set.sem, 2)
                g.affine_select(out=IDENT[:, :], in_=IDENT[:, :], compare_op=ALU.not_equal, fill=1.0, base=0,
                                pattern=[[-1, P]], channel_multiplier=1).then_inc(ident_set.sem, 1)

            def mask_x(i, b, c):
                pool.wait_ge(xin_in.sem, xin_in.at(b))
                pool.wait_ge(cbm_in.sem, cbm_in.at(b))
                pool.wait_ge(p0_full.sem, p0_full.at(b - 1))
                pool.wait_ge(w0_full.sem, w0_full.at(b - 2))
                g.tensor_tensor(XMC[:, c, :], XIN[:, c, :], CBM[:, :], ALU.mult).then_inc(xm_done.sem, 1)

            def masked_out(i, b):
                count_0 = held(pool, cbr_in.at(b))
                count_1 = held(pool, tq_full.at(b - 1))
                pool.wait_ge(ident_set.sem, 3)
                pool.wait_ge(cbr_in.sem, count_0)
                pool.wait_ge(tq_full.sem, count_1)
                g.tensor_scalar(CINV, CBR[:, :], -1.0, 1.0, ALU.mult, ALU.add).then_inc(cinv_done.sem, 1)

            def context0(i, b, q):
                pool.wait_ge(recip0_done.sem, recip0_done.at(b, 2 * q + 2))
                g.tensor_tensor(R0, R0, CBR[:, :], ALU.mult).then_inc(rc_done.sem, 1)
                pool.wait_ge(rc_done.sem, rc_done.at(b, q + 1))
                pool.wait_ge(context_taken, context.nth("AB"[q], i))
                g.tensor_tensor(TT, TT, R0, ALU.mult).then_inc(tt_done.sem, 1)
                pool.wait_ge(tt_done.sem, tt_done.at(b, q + 1))
                pool.wait_ge(m_done.sem, m_done.at(b, q + 1))
                g.tensor_tensor(XMC[:, q, :], XMC[:, q, :], TT, ALU.add).then_inc(ctx_done.sem, 1)

            def norm_heads(i, b, k):
                t, part = k // 2, k % 2
                rqk = RQK[:, t, part * H1:(part + 1) * H1]
                pool.wait_ge(msq_done.sem, msq_done.at(b, k + 1))
                g.tensor_tensor(rqk, rqk, HALF[:, :], ALU.pow).then_inc(rqk_done.sem, 1)
                pool.wait_ge(rqk_done.sem, rqk_done.at(b, k + 1))
                heads = QK[:, t, part * DM:(part + 1) * DM].rearrange("p (h d) -> p h d", d=DH)
                g.tensor_tensor(heads, heads, rqk.unsqueeze(2).broadcast_to([P, H1, DH]), ALU.mult) \
                    .then_inc(qn_done.sem, 1)

            def add_keys(i, b, c):
                if c == 0:
                    for h in range(QH):
                        pool.wait_ge(stack1_in[h].sem, stack1_in[h].at(b))
                if c >= 2:
                    pool.wait_ge(sum_done, probs.nth(("C", c - 2), i))
                pool.wait_ge(exp_done, scores.nth(("C", QH * c + QH - 1), i))
                e = E[:, probs.slot(("C", c)), :, :]
                g.tensor_tensor(key_sums(c), e[:, :, 0:N1], e[:, :, N1:2 * N1], ALU.add).then_inc(esum_done.sem, 1)

            def rstd(i, b):
                pool.wait_ge(ms_done.sem, ms_done.at(b))
                g.tensor_tensor(RSTD[:, :], RSTD[:, :], HALF[:, 0:2], ALU.pow).then_inc(rstd_done.sem, 1)

            def iteration(i):
                if has(i, -2):
                    add_keys(i - 1, i - 2, 3)
                if has(i, 1):
                    mask_x(i, i + 1, 0)
                    mask_x(i, i + 1, 1)
                if has(i, -1):
                    for k in range(4):
                        norm_heads(i, i - 1, k)
                if has(i, 0):
                    masked_out(i, i)
                    context0(i, i, 0)
                if has(i, -1):
                    add_keys(i, i - 1, 0)
                if has(i, 0):
                    context0(i, i, 1)
                if has(i, -1):
                    add_keys(i, i - 1, 1)
                    add_keys(i, i - 1, 2)
                if has(i, 0):
                    rstd(i, i)

            def no_modulation():
                pass

            identity()
            pipeline(pool, iteration, no_modulation)

        @block.sync
        def _(sp):
            def load_x(b):
                count_0 = held(sp, xm_done.at(b - 1))
                count_1 = held(sp, xs_done.at(b - 1))
                sp.wait_ge(ident_set.sem, 3)
                sp.wait_ge(xm_done.sem, count_0)
                sp.wait_ge(xs_done.sem, count_1)
                sp.dma_start(XIN[:, :, :], x_v[b]).then_inc(xin_in.sem, 16)
                sp.dma_start(CBM[:, :], cond[b].unsqueeze(0).partition_broadcast(P)).then_inc(cbm_in.sem, 16)

            def load_mask(b):
                count_0 = held(sp, ctx_done.at(b - 1))
                sp.wait_ge(ident_set.sem, 3)
                sp.wait_ge(ctx_done.sem, count_0)
                sp.dma_start(CBR[:, :], cond[b].unsqueeze(0).partition_broadcast(P)).then_inc(cbr_in.sem, 16)

            def load_residual(b):
                count_0 = held(sp, x1r_done.at(b - 1))
                count_1 = held(sp, y_done[0].at(b - 1))
                count_2 = held(sp, y_done[1].at(b - 1))
                sp.wait_ge(ident_set.sem, 3)
                sp.wait_ge(x1r_done.sem, count_0)
                sp.wait_ge(y_done[0].sem, count_1)
                sp.wait_ge(y_done[1].sem, count_2)
                sp.dma_start(X1[:, :, :], x_v[b]).then_inc(xres_in.sem, 16)

            def stack(dst_a, dst_b, a_hi, a_lo, b_hi, b_lo, event):
                for dst, src in ((dst_a[0:32], a_hi), (dst_a[32:64], a_lo), (dst_a[64:96], a_hi),
                                 (dst_b[0:32], b_hi), (dst_b[32:64], b_hi), (dst_b[64:96], b_lo)):
                    sp.dma_start(dst.bitcast(F32), src.bitcast(F32)).then_inc(event.sem, 16)

            def stack0(b, q):
                count_0 = held(sp, qhi_done.at(b, q + 1))
                count_1 = held(sp, qlo_done.at(b, q + 1))
                count_2 = held(sp, s0_full.at(b - 1, 16 * (q + 1)))
                sp.wait_ge(ident_set.sem, 3)
                sp.wait_ge(qhi_done.sem, count_0)
                sp.wait_ge(qlo_done.sem, count_1)
                sp.wait_ge(s0_full.sem, count_2)
                for hq in range(QH):
                    hi, lo = QHI[hq * DH:(hq + 1) * DH, q, :], QLO[hq * DH:(hq + 1) * DH, q, :]
                    h = q * QH + hq
                    stack(A0[:, h, :], B0[:, h, :], hi, lo, hi, lo, stack0_in[q][hq])

            def stack1(b):
                count_0 = held(sp, kqhi_done.at(b))
                count_1 = held(sp, other.nth_of_slot(("tq", 3), b + 1))
                count_2 = held(sp, s1_full.at(b - 1))
                sp.wait_ge(ident_set.sem, 3)
                sp.wait_ge(kqhi_done.sem, count_0)
                sp.wait_ge(taken(("tq", 3)), count_1)
                sp.wait_ge(s1_full.sem, count_2)
                for hq in range(QH):
                    own = slice(hq * DH, (hq + 1) * DH)
                    stack(A1[:, hq, :, :], B1[:, hq, :, :], KQHI[own, 1, :, :], KQLO[own, 1, :, :],
                          KQHI[own, 0, :, :], KQLO[own, 0, :, :], stack1_in[hq])

            def store(b):
                count_0 = held(sp, other.nth_of_slot(("w1", 1), b + 2))
                sp.wait_ge(ident_set.sem, 3)
                sp.wait_ge(taken(("w1", 1)), count_0)
                sp.dma_start(out_v[b], OUTT[:, :, :]).then_inc(stored.sem, 16)

            def iteration(i):
                if has(i, 0):
                    load_mask(i)
                if has(i, -1):
                    stack1(i - 1)
                if has(i, 1):
                    stack0(i + 1, 0)
                if has(i, -2):
                    store(i - 2)
                if has(i, 0):
                    load_residual(i)
                if has(i, 1):
                    stack0(i + 1, 1)
                if has(i, 2):
                    load_x(i + 2)

            def no_modulation():
                pass

            sp.dma_start(WQ[:, :, :], wq_t.rearrange("(c p) n -> p c n", p=P)).then_inc(wq_in.sem, 16)
            load_x(0)
            pipeline(sp, iteration, no_modulation)
            sp.wait_ge(stored.sem, 16 * NB)


def kernel(x, cond_2048, L0_cond_Wq, L0_cond_Wo, L1_cond_W_emb, L1_cond_b_emb, L1_cond_g_norm, L1_cond_W_qkv,
           L1_cond_g_q, L1_cond_g_k, L1_cond_W_out):
    import concourse.bacc as _bacc
    from concourse.bass_utils import run_bass_kernel_spmd as _run

    def by_partition(v, n):
        return np.ascontiguousarray(np.asarray(v).reshape(n, P).T)

    c = np.asarray(cond_2048)
    arrays = {
        "x": np.ascontiguousarray(x),
        "cond": np.ascontiguousarray(c),
        "cond_t": np.ascontiguousarray(c.reshape(NB, 4, P).transpose(2, 1, 0)),
        "wq_t": np.ascontiguousarray(np.asarray(L0_cond_Wq).T),
        "wo_t": np.ascontiguousarray(np.asarray(L0_cond_Wo).T),
        "w_emb": np.ascontiguousarray(L1_cond_W_emb),
        "b_emb_t": by_partition(L1_cond_b_emb, 8),
        "g_norm_t": by_partition(L1_cond_g_norm, 4),
        "w_qkv": np.ascontiguousarray(L1_cond_W_qkv),
        "g_q_t": np.ascontiguousarray(np.tile(np.asarray(L1_cond_g_q), QH).reshape(P, 1)),
        "g_k_t": np.ascontiguousarray(np.tile(np.asarray(L1_cond_g_k), QH).reshape(P, 1)),
        "w_out": np.ascontiguousarray(L1_cond_W_out),
    }
    nc = _bacc.Bacc("TRN2", target_bir_lowering=False, num_devices=1)
    args = [nc.dram_tensor(n, a.shape, F32, kind="ExternalInput").ap() for n, a in arrays.items()]
    args.append(nc.dram_tensor("out", (NB, D0, T0), F32, kind="ExternalOutput").ap())
    cond_resid(nc, *args)
    r = _run(nc, [arrays], core_ids=[0])
    return r.results[0]["out"]
```
